# Optimizing a Trainium2 kernel written in Bass

```python
import numpy as np
import jax
import jax.numpy as jnp

def _softmax(x, axis=-1):
    return jax.nn.softmax(x, axis=axis)

def _gelu(x):
    return jax.nn.gelu(x, approximate=True)

def _silu(x):
    return jax.nn.silu(x)

def _sigmoid(x):
    return jax.nn.sigmoid(x)

def _layernorm(x, axis=-1, eps=1e-05):
    m = jnp.mean(x, axis=axis, keepdims=True)
    v = jnp.var(x, axis=axis, keepdims=True)
    return (x - m) / jnp.sqrt(v + eps)

def _scatter_add(tgt, idx, src, axis=0):
    return tgt.at[idx].add(src)

def _segment_sum(src, seg, n):
    return jax.ops.segment_sum(src, seg, n)
kernel_name = 'mk_dlrm_tower_d1_rec_r8_dfcf14'

def setup_inputs(seed: int=0):
    np.random.seed(seed)
    _w = jnp.asarray

    def _rec_inputs():
        import jax
        import jax.numpy as jnp
        _tk = jax.random.key(seed)
        ids = jnp.stack([jax.random.randint(jax.random.fold_in(_tk, 200 + f), (512,), 0, v, jnp.int32) for f, v in enumerate([1250, 1000, 12500, 1000, 1250, 125000, 1000, 1000, 1250, 1250, 125000, 1250, 1250, 125000, 12500, 12500, 1000, 12500, 1000, 1000, 12500, 1000, 12500, 12500, 1250, 1250])], axis=1)
        tbl_0 = 0.05 * jax.random.normal(jax.random.fold_in(_tk, 500 + 0), (1250, 64), jnp.float32)
        tbl_1 = 0.05 * jax.random.normal(jax.random.fold_in(_tk, 500 + 1), (1000, 64), jnp.float32)
        tbl_2 = 0.05 * jax.random.normal(jax.random.fold_in(_tk, 500 + 2), (12500, 64), jnp.float32)
        tbl_3 = 0.05 * jax.random.normal(jax.random.fold_in(_tk, 500 + 3), (1000, 64), jnp.float32)
        tbl_4 = 0.05 * jax.random.normal(jax.random.fold_in(_tk, 500 + 4), (1250, 64), jnp.float32)
        tbl_5 = 0.05 * jax.random.normal(jax.random.fold_in(_tk, 500 + 5), (125000, 64), jnp.float32)
        tbl_6 = 0.05 * jax.random.normal(jax.random.fold_in(_tk, 500 + 6), (1000, 64), jnp.float32)
        tbl_7 = 0.05 * jax.random.normal(jax.random.fold_in(_tk, 500 + 7), (1000, 64), jnp.float32)
        tbl_8 = 0.05 * jax.random.normal(jax.random.fold_in(_tk, 500 + 8), (1250, 64), jnp.float32)
        tbl_9 = 0.05 * jax.random.normal(jax.random.fold_in(_tk, 500 + 9), (1250, 64), jnp.float32)
        tbl_10 = 0.05 * jax.random.normal(jax.random.fold_in(_tk, 500 + 10), (125000, 64), jnp.float32)
        tbl_11 = 0.05 * jax.random.normal(jax.random.fold_in(_tk, 500 + 11), (1250, 64), jnp.float32)
        tbl_12 = 0.05 * jax.random.normal(jax.random.fold_in(_tk, 500 + 12), (1250, 64), jnp.float32)
        tbl_13 = 0.05 * jax.random.normal(jax.random.fold_in(_tk, 500 + 13), (125000, 64), jnp.float32)
        tbl_14 = 0.05 * jax.random.normal(jax.random.fold_in(_tk, 500 + 14), (12500, 64), jnp.float32)
        tbl_15 = 0.05 * jax.random.normal(jax.random.fold_in(_tk, 500 + 15), (12500, 64), jnp.float32)
        tbl_16 = 0.05 * jax.random.normal(jax.random.fold_in(_tk, 500 + 16), (1000, 64), jnp.float32)
        tbl_17 = 0.05 * jax.random.normal(jax.random.fold_in(_tk, 500 + 17), (12500, 64), jnp.float32)
        tbl_18 = 0.05 * jax.random.normal(jax.random.fold_in(_tk, 500 + 18), (1000, 64), jnp.float32)
        tbl_19 = 0.05 * jax.random.normal(jax.random.fold_in(_tk, 500 + 19), (1000, 64), jnp.float32)
        tbl_20 = 0.05 * jax.random.normal(jax.random.fold_in(_tk, 500 + 20), (12500, 64), jnp.float32)
        tbl_21 = 0.05 * jax.random.normal(jax.random.fold_in(_tk, 500 + 21), (1000, 64), jnp.float32)
        tbl_22 = 0.05 * jax.random.normal(jax.random.fold_in(_tk, 500 + 22), (12500, 64), jnp.float32)
        tbl_23 = 0.05 * jax.random.normal(jax.random.fold_in(_tk, 500 + 23), (12500, 64), jnp.float32)
        tbl_24 = 0.05 * jax.random.normal(jax.random.fold_in(_tk, 500 + 24), (1250, 64), jnp.float32)
        tbl_25 = 0.05 * jax.random.normal(jax.random.fold_in(_tk, 500 + 25), (1250, 64), jnp.float32)
        _rk = jax.random.fold_in(_tk, 7)
        r_dense_t = 7.22013e-05 + 1.00017 * jax.random.normal(jax.random.fold_in(_rk, 101), (512, 256), jnp.float32)
        W_top1 = 0.0360844 * jax.random.normal(jax.random.fold_in(_tk, 801), (768, 512), jnp.float32)
        W_top2 = 0.0441942 * jax.random.normal(jax.random.fold_in(_tk, 802), (512, 256), jnp.float32)
        W_top3 = 0.0625 * jax.random.normal(jax.random.fold_in(_tk, 803), (256, 1), jnp.float32)
        b_top1 = jnp.zeros((512,), jnp.float32)
        b_top2 = jnp.zeros((256,), jnp.float32)
        return (r_dense_t, ids, tbl_0, tbl_1, tbl_2, tbl_3, tbl_4, tbl_5, tbl_6, tbl_7, tbl_8, tbl_9, tbl_10, tbl_11, tbl_12, tbl_13, tbl_14, tbl_15, tbl_16, tbl_17, tbl_18, tbl_19, tbl_20, tbl_21, tbl_22, tbl_23, tbl_24, tbl_25, W_top1, b_top1, W_top2, b_top2, W_top3)
    r_dense_t, ids, tbl_0, tbl_1, tbl_2, tbl_3, tbl_4, tbl_5, tbl_6, tbl_7, tbl_8, tbl_9, tbl_10, tbl_11, tbl_12, tbl_13, tbl_14, tbl_15, tbl_16, tbl_17, tbl_18, tbl_19, tbl_20, tbl_21, tbl_22, tbl_23, tbl_24, tbl_25, W_top1, b_top1, W_top2, b_top2, W_top3 = _rec_inputs()

    def _L0_rec_setup():
        import jax, jax.numpy as jnp
        import numpy as np
        EPS = 1e-05
        NI = 33
        TRIL_I, TRIL_J = np.tril_indices(NI, k=-1)

        def layer_norm(x, g, b):
            m = jnp.mean(x, axis=-1, keepdims=True)
            v = jnp.mean(jnp.square(x - m), axis=-1, keepdims=True)
            return (x - m) * jax.lax.rsqrt(v + EPS) * g + b
        key = jax.random.key(seed)
        ks = jax.random.split(key, 8)
        B, D_DENSE, N_SP, D_SP = (4096, 256, 26, 64)
        E, PROJ, MAXD, NFLAT = (128, 32, 512, 528)
        dense_t = jax.random.normal(ks[0], (B, D_DENSE), dtype=jnp.float32)
        sparse_t = jax.random.normal(ks[1], (B, N_SP, D_SP), dtype=jnp.float32)
        Wd = jax.random.normal(ks[2], (E, D_DENSE), dtype=jnp.float32) / np.sqrt(D_DENSE)
        Ws = jax.random.normal(ks[3], (E, D_SP), dtype=jnp.float32) / np.sqrt(D_SP)
        Wsi = jax.random.normal(ks[4], (PROJ, N_SP), dtype=jnp.float32) / np.sqrt(N_SP)
        Wl = jax.random.normal(ks[5], (MAXD, NFLAT), dtype=jnp.float32) / np.sqrt(NFLAT)
        gd = jnp.ones((E,), jnp.float32)
        bd = jnp.zeros((E,), jnp.float32)
        gs = jnp.ones((E,), jnp.float32)
        bs = jnp.zeros((E,), jnp.float32)
        gsi = jnp.ones((PROJ,), jnp.float32)
        bsi = jnp.zeros((PROJ,), jnp.float32)
        gl = jnp.ones((MAXD,), jnp.float32)
        bl = jnp.zeros((MAXD,), jnp.float32)
        return {'dense_t': dense_t, 'sparse_t': sparse_t, 'Wd': Wd, 'gd': gd, 'bd': bd, 'Ws': Ws, 'gs': gs, 'bs': bs, 'Wsi': Wsi, 'gsi': gsi, 'bsi': bsi, 'Wl': Wl, 'gl': gl, 'bl': bl, 'dims_in_use': 384}
    _L0_rec_all = _L0_rec_setup()
    _L0_rec_in = {k: v for k, v in _L0_rec_all.items() if k in ('Wd', 'gd', 'bd', 'Ws', 'gs', 'bs', 'Wsi', 'gsi', 'bsi', 'Wl', 'gl', 'bl')}
    del _L0_rec_all
    return {'r_dense_t': r_dense_t, 'ids': ids, 'tbl_0': tbl_0, 'tbl_1': tbl_1, 'tbl_2': tbl_2, 'tbl_3': tbl_3, 'tbl_4': tbl_4, 'tbl_5': tbl_5, 'tbl_6': tbl_6, 'tbl_7': tbl_7, 'tbl_8': tbl_8, 'tbl_9': tbl_9, 'tbl_10': tbl_10, 'tbl_11': tbl_11, 'tbl_12': tbl_12, 'tbl_13': tbl_13, 'tbl_14': tbl_14, 'tbl_15': tbl_15, 'tbl_16': tbl_16, 'tbl_17': tbl_17, 'tbl_18': tbl_18, 'tbl_19': tbl_19, 'tbl_20': tbl_20, 'tbl_21': tbl_21, 'tbl_22': tbl_22, 'tbl_23': tbl_23, 'tbl_24': tbl_24, 'tbl_25': tbl_25, 'W_top1': W_top1, 'b_top1': b_top1, 'W_top2': W_top2, 'b_top2': b_top2, 'W_top3': W_top3, 'L0_rec_Wd': _L0_rec_in['Wd'], 'L0_rec_gd': _L0_rec_in['gd'], 'L0_rec_bd': _L0_rec_in['bd'], 'L0_rec_Ws': _L0_rec_in['Ws'], 'L0_rec_gs': _L0_rec_in['gs'], 'L0_rec_bs': _L0_rec_in['bs'], 'L0_rec_Wsi': _L0_rec_in['Wsi'], 'L0_rec_gsi': _L0_rec_in['gsi'], 'L0_rec_bsi': _L0_rec_in['bsi'], 'L0_rec_Wl': _L0_rec_in['Wl'], 'L0_rec_gl': _L0_rec_in['gl'], 'L0_rec_bl': _L0_rec_in['bl']}

def reference(r_dense_t, ids, tbl_0, tbl_1, tbl_2, tbl_3, tbl_4, tbl_5, tbl_6, tbl_7, tbl_8, tbl_9, tbl_10, tbl_11, tbl_12, tbl_13, tbl_14, tbl_15, tbl_16, tbl_17, tbl_18, tbl_19, tbl_20, tbl_21, tbl_22, tbl_23, tbl_24, tbl_25, W_top1, b_top1, W_top2, b_top2, W_top3, L0_rec_Wd, L0_rec_gd, L0_rec_bd, L0_rec_Ws, L0_rec_gs, L0_rec_bs, L0_rec_Wsi, L0_rec_gsi, L0_rec_bsi, L0_rec_Wl, L0_rec_gl, L0_rec_bl):
    import jax
    import jax.numpy as jnp

    def _L0_rec_ref(dense_t, sparse_t, Wd, gd, bd, Ws, gs, bs, Wsi, gsi, bsi, Wl, gl, bl, dims_in_use):
        import jax, jax.numpy as jnp
        import numpy as np
        EPS = 1e-05
        NI = 33
        TRIL_I, TRIL_J = np.tril_indices(NI, k=-1)

        def layer_norm(x, g, b):
            m = jnp.mean(x, axis=-1, keepdims=True)
            v = jnp.mean(jnp.square(x - m), axis=-1, keepdims=True)
            return (x - m) * jax.lax.rsqrt(v + EPS) * g + b
        x = layer_norm(dense_t @ Wd.T, gd, bd)
        y = layer_norm(jnp.einsum('bnd,ed->bne', sparse_t, Ws), gs, bs)
        y = jnp.einsum('bne,pn->bep', y, Wsi)
        y = layer_norm(y, gsi, bsi)
        y = jnp.swapaxes(y, 1, 2)
        T = jnp.concatenate([x[:, None, :], y], axis=1)
        Z = jnp.einsum('bnd,bmd->bnm', T, T)
        Zflat = Z[:, TRIL_I, TRIL_J]
        out = layer_norm(Zflat @ Wl.T, gl, bl)
        maxd = out.shape[-1]
        mask = (jnp.arange(maxd) < dims_in_use).astype(out.dtype)
        return out * mask
    e = jnp.stack([tbl_0[ids[:, 0]], tbl_1[ids[:, 1]], tbl_2[ids[:, 2]], tbl_3[ids[:, 3]], tbl_4[ids[:, 4]], tbl_5[ids[:, 5]], tbl_6[ids[:, 6]], tbl_7[ids[:, 7]], tbl_8[ids[:, 8]], tbl_9[ids[:, 9]], tbl_10[ids[:, 10]], tbl_11[ids[:, 11]], tbl_12[ids[:, 12]], tbl_13[ids[:, 13]], tbl_14[ids[:, 14]], tbl_15[ids[:, 15]], tbl_16[ids[:, 16]], tbl_17[ids[:, 17]], tbl_18[ids[:, 18]], tbl_19[ids[:, 19]], tbl_20[ids[:, 20]], tbl_21[ids[:, 21]], tbl_22[ids[:, 22]], tbl_23[ids[:, 23]], tbl_24[ids[:, 24]], tbl_25[ids[:, 25]]], axis=1)
    z = _L0_rec_ref(r_dense_t, e, L0_rec_Wd, L0_rec_gd, L0_rec_bd, L0_rec_Ws, L0_rec_gs, L0_rec_bs, L0_rec_Wsi, L0_rec_gsi, L0_rec_bsi, L0_rec_Wl, L0_rec_gl, L0_rec_bl, 384)
    z = z.reshape(z.shape[0], -1)
    h = jnp.concatenate([z, r_dense_t], axis=1)
    h = jnp.maximum(h @ W_top1 + b_top1, 0.0)
    h = jnp.maximum(h @ W_top2 + b_top2, 0.0)
    y = h @ W_top3
    return y

_drawn_inputs = setup_inputs


def setup_inputs(seed=0):
    import zlib

    import numpy as np

    out = dict(_drawn_inputs(seed))
    spreads = {'b_top1': (0.0, 0.1),
     'b_top2': (0.0, 0.1),
     'L0_rec_gd': (1.0, 0.6),
     'L0_rec_bd': (0.0, 0.8),
     'L0_rec_gs': (1.0, 0.6),
     'L0_rec_bs': (0.0, 0.1),
     'L0_rec_gsi': (1.0, 0.2),
     'L0_rec_bsi': (0.0, 0.1),
     'L0_rec_gl': (1.0, 0.2),
     'L0_rec_bl': (0.0, 0.1)}
    factors = {}
    for name, (base, spread) in spreads.items():
        noise = np.random.default_rng([zlib.crc32(name.encode()), seed]).standard_normal(out[name].shape)
        drawn = base * np.exp(spread * noise) if base else spread * noise
        out[name] = jnp.asarray(drawn.astype(out[name].dtype))
    for name, factor in factors.items():
        out[name] = (out[name] * factor).astype(out[name].dtype)
    return out
```

```python
from contextlib import ExitStack

import numpy as np

import concourse.bass as bass
from concourse import mybir

ALU = mybir.AluOpType
ACT = mybir.ActivationFunctionType
AX = mybir.AxisListType
F32 = mybir.dt.float32
BF16 = mybir.dt.bfloat16
I32 = mybir.dt.int32

P = 128
EPS = 1e-5
B = 512
NT = 26
D = 64
E = 128
PR = 32
NI = PR + 1
DD = 256
MD = 512
USED = 384
H1, H2 = 512, 256
TILES = B // P
CH = NT * P // P
PAIRS = CH // 2
PERIOD = CH // 2
SPC = 6
SPB = 512 // PR
BANKS = P // SPB
J, G = 4, P // 4
QA, QB = 4, 9
GZ = 8
ZSTEPS = G // GZ
PARTS = 3
DK, HK, ZK = DD // P, H1 // P, USED // P
VOCAB = [1250, 1000, 12500, 1000, 1250, 125000, 1000, 1000, 1250, 1250, 125000, 1250, 1250,
         125000, 12500, 12500, 1000, 12500, 1000, 1000, 12500, 1000, 12500, 12500, 1250, 1250]


def chunk_samples(c):
    return P * c // NT, (P * c + P - 1) // NT


def bank_pieces(k):
    half, kb = divmod(k, BANKS // 2)
    pieces = []
    for c in range(PERIOD):
        s0, s1 = chunk_samples(c)
        a, b = max(s0, SPB * kb), min(s1, SPB * kb + SPB - 1)
        if a <= b:
            pieces.append((half * PERIOD + c, a - s0, a - SPB * kb, b - a + 1))
    return pieces


def pair_of_bank(k):
    return bank_pieces(k)[-1][0] // 2


def build(nc, rows_at, table_base, tables, dense, wd, gd, bd, ws, gs, bs, wsi_blocks, wsi_t, gsi, bsi,
          wl_slots, gl, bl, w1, b1, w2, b2, w3, eye, part_masks, y_out):
    with ExitStack() as ctx:
        def sb(name, shape, dt=F32):
            return ctx.enter_context(nc.sbuf_tensor(name, shape, dt))

        def psum(name, shape):
            return ctx.enter_context(nc.psum_tensor(name, shape, F32))

        def sem(name):
            return ctx.enter_context(nc.semaphore(name))

        rows_sb = sb("rows_sb", [P, TILES * CH], I32)
        base_sb = sb("base_sb", [P, TILES * CH], I32)
        row_index = sb("row_index", [P, (TILES + 1) * CH], I32)
        tile_index = sb("tile_index", [P, CH], I32)
        eye_sb = sb("eye_sb", [P, P])
        ws_raw = sb("ws_raw", [P, 2, E])
        ws_mean = sb("ws_mean", [P, 2])
        ws_c = sb("ws_c", [P, 2, E])
        gs_sb = sb("gs_sb", [P, E])
        wsi_raw = sb("wsi_raw", [P, PERIOD * SPC, PR])
        wsi_mean = sb("wsi_mean", [P, PERIOD * SPC])
        wsi_c = sb("wsi_c", [P, PERIOD * SPC, PR])
        wsit_raw = sb("wsit_raw", [NT, PR])
        wsit_mean = sb("wsit_mean", [NT, 1])
        wsit_c = sb("wsit_c", [NT, PR])
        ones_sb = sb("ones_sb", [NT, PARTS * PARTS])
        masks_sb = sb("masks_sb", [PARTS * PARTS, 2 * PARTS])
        bs_sb = sb("bs_sb", [PARTS * PARTS, E])
        sc_sb = sb("sc_sb", [PARTS * PARTS, PR])
        bs_parts = sb("bs_parts", [PARTS * PARTS, E], BF16)
        sc_parts = sb("sc_parts", [PARTS * PARTS, PR], BF16)
        split_hi = sb("split_hi", [PARTS * PARTS, 2, PARTS, E], BF16)
        split_f = sb("split_f", [PARTS * PARTS, 2, 4, E])
        gsi_sb = sb("gsi_sb", [P, PR])
        bsi_sb = sb("bsi_sb", [P, PR])
        wl_sb = sb("wl_sb", [P, QB, MD])
        gl_sb = sb("gl_sb", [P, ZK])
        bl_sb = sb("bl_sb", [P, ZK])
        w1_sb = sb("w1_sb", [P, ZK + DK, H1])
        b1_sb = sb("b1_sb", [P, HK])
        w2_sb = sb("w2_sb", [P, HK, H2])
        b2_sb = sb("b2_sb", [P, H2 // P])
        w3_sb = sb("w3_sb", [P, H2 // P])
        gd_sb = sb("gd_sb", [P, 1])
        bd_sb = sb("bd_sb", [P, 1])
        wd_sb = sb("wd_sb", [P, DK, E])
        eps_sb = sb("eps_sb", [P, 1])
        dense_sb = sb("dense_sb", [P, DK, B])
        x_stats = sb("x_stats", [P, TILES, 6])
        x_mv = sb("x_mv", [P, TILES, 2])
        x_std = sb("x_std", [P, TILES])
        x_rstd = sb("x_rstd", [P, TILES])
        x_hat = sb("x_hat", [P, TILES, E])
        x_t = sb("x_t", [P, TILES, G, J])
        emb = sb("emb", [P, CH, D])
        emb_t = sb("emb_t", [P, PAIRS, P])
        sq_junk = sb("sq_junk", [P, 2, E])
        y_var = sb("y_var", [P, CH])
        y_std = sb("y_std", [P, CH])
        y_rstd = sb("y_rstd", [P, CH])
        y_norm = sb("y_norm", [P, CH, E])
        proj_sq = sb("proj_sq", [P, 2, SPB * PR])
        p_var = sb("p_var", [P, BANKS, SPB])
        p_std = sb("p_std", [P, BANKS, SPB])
        p_rstd = sb("p_rstd", [P, BANKS, SPB])
        p_hat = sb("p_hat", [P, P, PR])
        items = sb("items", [P, P, NI])
        z_jp = sb("z_jp", [P, QA, G, QB])
        z_qp = sb("z_qp", [P, J, G, QB])
        o_stats = sb("o_stats", [P, 6])
        o_mv = sb("o_mv", [P, 2])
        o_std = sb("o_std", [P, 1])
        o_rstd = sb("o_rstd", [P, 1])
        o_hat = sb("o_hat", [P, USED])
        z_t = sb("z_t", [P, ZK, P])
        h1_t = sb("h1_t", [P, HK, P])
        h2_t = sb("h2_t", [P, H2 // P, P])
        y_sb = sb("y_sb", [1, TILES, G, J])

        ps_t = [psum(f"ps_t{r}", [P, P]) for r in range(2)]
        ps_y = [psum(f"ps_y{r}", [P, 2, E]) for r in range(2)]
        ps_p = [psum(f"ps_p{r}", [P, SPB * PR]) for r in range(2)]
        ps_z = psum("ps_z", [P, 512])
        ps_m = psum("ps_m", [P, 512])

        rows_loaded = sem("rows_loaded")
        small_loaded = sem("small_loaded")
        wsi_loaded = sem("wsi_loaded")
        x_loaded = sem("x_loaded")
        wl_loaded = sem("wl_loaded")
        top_loaded = sem("top_loaded")
        index_ready = sem("index_ready")
        dve_prep = sem("dve_prep")
        weights_ready = sem("weights_ready")
        sc_summed = sem("sc_summed")
        x_projected = sem("x_projected")
        x_std_ready = sem("x_std_ready")
        x_stats_ready = sem("x_stats_ready")
        x_hat_ready = sem("x_hat_ready")
        x_turned = sem("x_turned")
        x_ready = sem("x_ready")
        gathered = [sem(f"gathered{c}") for c in range(CH)]
        pair_turned = sem("pair_turned")
        pair_copied = sem("pair_copied")
        pair_embedded = sem("pair_embedded")
        y_squared = sem("y_squared")
        y_std_ready = sem("y_std_ready")
        y_rstd_ready = sem("y_rstd_ready")
        y_normed = sem("y_normed")
        bank_projected = sem("bank_projected")
        bank_squared = sem("bank_squared")
        p_var_ready = sem("p_var_ready")
        p_std_ready = sem("p_std_ready")
        p_rstd_ready = sem("p_rstd_ready")
        p_hat_ready = sem("p_hat_ready")
        items_ready = sem("items_ready")
        z_ready = sem("z_ready")
        z_copied = sem("z_copied")
        z_regrouped = sem("z_regrouped")
        o_ready = sem("o_ready")
        o_stats_ready = sem("o_stats_ready")
        o_mv_ready = sem("o_mv_ready")
        o_std_ready = sem("o_std_ready")
        o_rstd_ready = sem("o_rstd_ready")
        o_hat_ready = sem("o_hat_ready")
        o_turned = sem("o_turned")
        z_t_ready = sem("z_t_ready")
        h1_summed = sem("h1_summed")
        h1_ready = sem("h1_ready")
        h2_summed = sem("h2_summed")
        h2_ready = sem("h2_ready")
        y_summed = sem("y_summed")
        y_copied = sem("y_copied")
        y_stored = sem("y_stored")

        SMALL = 11
        HALVES = ((0, 7), (7, PAIRS))
        TOP = 7
        block = ctx.enter_context(nc.Block())

        @block.sync
        def _(sp):
            sp.dma_start(rows_sb[:], rows_at).then_inc(rows_loaded, 16)
            sp.dma_start(base_sb[:], table_base).then_inc(rows_loaded, 16)
            sp.dma_start(eye_sb[:], eye).then_inc(small_loaded, 16)
            sp.dma_start(ws_raw[:], ws).then_inc(small_loaded, 16)
            sp.dma_start(gs_sb[:], gs.partition_broadcast(P)).then_inc(small_loaded, 16)
            sp.dma_start(wsi_raw[:].rearrange("p a b -> p (a b)"), wsi_blocks).then_inc(wsi_loaded, 16)
            sp.dma_start(wsit_raw[:], wsi_t).then_inc(small_loaded, 16)
            sp.dma_start(masks_sb[:], part_masks).then_inc(small_loaded, 16)
            sp.dma_start(bs_sb[:], bs.partition_broadcast(PARTS * PARTS)).then_inc(small_loaded, 16)
            sp.dma_start(gsi_sb[:], gsi.partition_broadcast(P)).then_inc(small_loaded, 16)
            sp.dma_start(bsi_sb[:], bsi.partition_broadcast(P)).then_inc(small_loaded, 16)
            sp.dma_start(gd_sb[:], gd).then_inc(small_loaded, 16)
            sp.dma_start(bd_sb[:], bd).then_inc(small_loaded, 16)
            sp.dma_start(gl_sb[:], gl).then_inc(small_loaded, 16)
            sp.dma_start(dense_sb[:], dense).then_inc(x_loaded, 16)
            sp.dma_start(wd_sb[:], wd).then_inc(x_loaded, 16)
            sp.dma_start(wl_sb[:], wl_slots).then_inc(wl_loaded, 16)
            sp.dma_start(bl_sb[:], bl).then_inc(top_loaded, 16)
            sp.dma_start(w1_sb[:], w1).then_inc(top_loaded, 16)
            sp.dma_start(b1_sb[:], b1).then_inc(top_loaded, 16)
            sp.dma_start(w2_sb[:], w2).then_inc(top_loaded, 16)
            sp.dma_start(b2_sb[:], b2).then_inc(top_loaded, 16)
            sp.dma_start(w3_sb[:, 0:1], w3[0]).then_inc(top_loaded, 16)
            sp.dma_start(w3_sb[:, 1:2], w3[1]).then_inc(top_loaded, 16)

            def regroup(i, first):
                sp.wait_ge(z_copied, ZSTEPS * (i + 1))
                if not first:
                    sp.wait_ge(o_ready, i)
                for j in range(J):
                    for qa in range(QA):
                        sp.dma_start(z_qp[PR * qa:PR * qa + PR, j, :, :],
                                     z_jp[PR * j:PR * j + PR, qa, :, :]
                                     ).then_inc(z_regrouped, 16)

            regroup(0, True)
            with sp.Fori(1, TILES) as i:
                regroup(i, False)
            sp.wait_ge(y_copied, TILES)
            sp.dma_start(y_out, y_sb[:].rearrange("p a b c -> p (a b c)")).then_inc(y_stored, 16)
            sp.wait_ge(y_stored, 16)

        @block.gpsimd
        def _(pool):
            halves = pool.alloc_register("halves")
            pool.reg_mov(halves, 1)

            def gather():
                for c in range(CH):
                    for half, (lo, hi) in enumerate(HALVES):
                        if c == 2 * lo:
                            pool.wait_ge(index_ready, halves)
                            pool.reg_add(halves, halves, 1)
                    pool.indirect_dma_start(
                        out=emb[:, c, :], out_offset=None, in_=tables,
                        in_offset=bass.IndirectOffsetOnAxis(
                            ap=tile_index[:, c:c + 1], axis=0),
                    ).then_inc(gathered[c], 16)

            with pool.Fori(0, TILES):
                gather()

        @block.scalar
        def _(act):
            act.wait_ge(weights_ready, 1)
            for t in range(TILES):
                act.wait_ge(x_stats_ready, t + 1)
                nc.scalar.activation(x_std[:, t:t + 1], x_mv[:, t, 1:2], ACT.Sqrt,
                                     bias=eps_sb[:, 0:1]).then_inc(x_std_ready, 1)
            act.wait_ge(x_turned, TILES)
            for t in range(TILES):
                nc.scalar.activation(x_t[:, t].rearrange("p g j -> p j g"),
                                     ps_z[:, t * P:(t + 1) * P].rearrange("p (j g) -> p j g", j=J),
                                     ACT.Identity, bias=bd_sb[:, 0:1], scale=gd_sb[:, 0:1]
                                     ).then_inc(x_ready, 1)

            def copy_pair(i, t, first):
                n = PAIRS * i + t
                act.wait_ge(pair_turned, n + 1)
                if not first:
                    act.wait_ge(pair_embedded, n - PAIRS + 1)
                nc.scalar.copy(emb_t[:, t, :], ps_t[t % 2][:]).then_inc(pair_copied, 1)

            def square_pair(i, t, first):
                n = PAIRS * i + t
                act.wait_ge(pair_embedded, n + 1)
                if not first:
                    act.wait_ge(y_std_ready, n - PAIRS + 1)
                for r in range(2):
                    if t >= 1 or not first:
                        act.wait_ge(y_squared, 2 * (n - 1) + r + 1)
                    nc.scalar.activation(sq_junk[:, r, :], ps_y[t % 2][:, r, :], ACT.Square,
                                         scale=float(E) ** -0.5,
                                         accum_out=y_var[:, 2 * t + r:2 * t + r + 1]
                                         ).then_inc(y_squared, 1)
                act.wait_ge(y_squared, 2 * n + 2)
                if not first:
                    act.wait_ge(y_rstd_ready, n - PAIRS + 1)
                nc.scalar.activation(y_std[:, 2 * t:2 * t + 2], y_var[:, 2 * t:2 * t + 2], ACT.Sqrt,
                                     bias=eps_sb[:, 0:1]).then_inc(y_std_ready, 1)

            def square_bank(i, k, first):
                m = BANKS * i + k
                act.wait_ge(bank_projected, m + 1)
                if k >= 2 or not first:
                    act.wait_ge(p_var_ready, m - 1)
                nc.scalar.activation(proj_sq[:, k % 2, :], ps_p[k % 2][:], ACT.Square,
                                     scale=float(PR) ** -0.5).then_inc(bank_squared, 1)

            def std_bank(i, k, first):
                m = BANKS * i + k
                act.wait_ge(p_var_ready, m + 1)
                if not first:
                    act.wait_ge(p_rstd_ready, m - BANKS + 1)
                nc.scalar.activation(p_std[:, k, :], p_var[:, k, :], ACT.Sqrt,
                                     bias=eps_sb[:, 0:1]).then_inc(p_std_ready, 1)

            def std_out(i):
                act.wait_ge(o_mv_ready, i + 1)
                nc.scalar.activation(o_std[:], o_mv[:, 1:2], ACT.Sqrt,
                                     bias=eps_sb[:, 0:1]).then_inc(o_std_ready, 1)

            def scale_z(i):
                act.wait_ge(o_turned, i + 1)
                for c in range(ZK):
                    nc.scalar.activation(z_t[:, c, :], ps_m[:, c * P:(c + 1) * P], ACT.Identity,
                                         bias=bl_sb[:, c:c + 1], scale=gl_sb[:, c:c + 1]
                                         ).then_inc(z_t_ready, 1)

            def relu_1(i):
                act.wait_ge(h1_summed, i + 1)
                for c in range(HK):
                    nc.scalar.activation(h1_t[:, c, :], ps_m[:, c * P:(c + 1) * P], ACT.Relu,
                                         bias=b1_sb[:, c:c + 1]).then_inc(h1_ready, 1)

            def relu_2(i):
                act.wait_ge(h2_summed, i + 1)
                for c in range(H2 // P):
                    nc.scalar.activation(h2_t[:, c, :], ps_m[:, c * P:(c + 1) * P], ACT.Relu,
                                         bias=b2_sb[:, c:c + 1]).then_inc(h2_ready, 1)

            def copy_y(i):
                act.wait_ge(y_summed, i + 1)
                nc.scalar.copy(y_sb[0:1, bass.ds(i, 1)].rearrange("p a g j -> p a j g"),
                               ps_m[0:1, 0:P].rearrange("p (a j g) -> p a j g", a=1, j=J)
                               ).then_inc(y_copied, 1)

            def front_step(i, t, first):
                if t < PAIRS:
                    copy_pair(i, t, first)
                if 1 <= t <= PAIRS:
                    square_pair(i, t - 1, first)
                for k in range(BANKS):
                    if pair_of_bank(k) == t - 3:
                        square_bank(i, k, first)
                    if pair_of_bank(k) == t - 4:
                        std_bank(i, k, first)

            def back_step(i, t):
                if t == 11:
                    act.wait_ge(top_loaded, 16 * TOP)
                    std_out(i)
                    scale_z(i)
                if t == 12:
                    relu_1(i)
                if t == 14:
                    relu_2(i)
                    copy_y(i)

            for t in range(PAIRS + 4):
                front_step(0, t, True)
            with act.Fori(1, TILES) as i:
                for t in range(PAIRS + 4):
                    front_step(i, t, False)
                    back_step(i - 1, t)
            for t in range(PAIRS + 4):
                back_step(TILES - 1, t)

        @block.vector
        def _(dve):
            chain = [0]

            def link(ins):
                chain[0] += 1
                ins.then_inc(dve_prep, 1)
                dve.wait_ge(dve_prep, chain[0])

            dve.wait_ge(rows_loaded, 32)
            nc.vector.memset(row_index[:, TILES * CH:], 0)
            link(nc.vector.tensor_tensor(row_index[:, 0:TILES * CH], rows_sb[:], base_sb[:], ALU.add))
            nc.vector.tensor_copy(tile_index[:], row_index[:, 0:CH]).then_inc(index_ready, len(HALVES))
            nc.vector.memset(z_jp[:, QA - 1, :, NI - (QA - 1) * QB:QB], 0.0)
            nc.vector.memset(ones_sb[:], 1.0)
            link(nc.vector.memset(eps_sb[:], EPS))
            dve.wait_ge(small_loaded, 16 * SMALL)
            link(nc.vector.tensor_reduce(ws_mean[:], ws_raw[:], AX.X, ALU.add))
            link(nc.vector.tensor_scalar(ws_mean[:], ws_mean[:], 1.0 / E, None, ALU.mult))
            link(nc.vector.tensor_tensor(ws_c[:], ws_raw[:],
                                         ws_mean[:].rearrange("p (a b) -> p a b", b=1).broadcast_to([P, 2, E]),
                                         ALU.subtract))
            link(nc.vector.tensor_reduce(wsit_mean[:], wsit_raw[:], AX.X, ALU.add))
            link(nc.vector.tensor_scalar(wsit_mean[:], wsit_mean[:], 1.0 / PR, None, ALU.mult))
            link(nc.vector.tensor_scalar(wsit_c[:], wsit_raw[:], wsit_mean[:, 0:1], None, ALU.subtract))
            nc.vector.tensor_copy(wsit_mean[:], wsit_mean[:]).then_inc(weights_ready, 1)
            dve.wait_ge(wsi_loaded, 16)
            link(nc.vector.tensor_reduce(wsi_mean[:], wsi_raw[:], AX.X, ALU.add))
            link(nc.vector.tensor_scalar(wsi_mean[:], wsi_mean[:], 1.0 / PR, None, ALU.mult))
            link(nc.vector.tensor_tensor(wsi_c[:], wsi_raw[:],
                                         wsi_mean[:].rearrange("p (a b) -> p a b", b=1).broadcast_to(
                                             [P, PERIOD * SPC, PR]), ALU.subtract))
            dve.wait_ge(sc_summed, 1)
            link(nc.vector.tensor_copy(sc_sb[:], ps_m[0:PARTS * PARTS, 0:PR]))
            for side, (src, dst, n) in enumerate(((bs_sb, bs_parts, E), (sc_sb, sc_parts, PR))):
                rest = src[:, 0:n]
                total = None
                for q in range(PARTS):
                    hi = split_hi[:, side, q, 0:n]
                    link(nc.vector.tensor_copy(hi, rest))
                    if q < PARTS - 1:
                        link(nc.vector.tensor_tensor(split_f[:, side, q, 0:n], rest, hi, ALU.subtract))
                        rest = split_f[:, side, q, 0:n]
                    mask = masks_sb[:, PARTS * side + q:PARTS * side + q + 1]
                    into = dst[:, 0:n] if q == PARTS - 1 else split_f[:, side, 2 + q, 0:n]
                    if total is None:
                        link(nc.vector.tensor_scalar(into, hi, mask, None, ALU.mult))
                    else:
                        link(nc.vector.scalar_tensor_tensor(out=into, in0=hi, scalar=mask, in1=total,
                                                            op0=ALU.mult, op1=ALU.add))
                    total = into
            nc.vector.tensor_copy(wsit_mean[:], wsit_mean[:]).then_inc(weights_ready, 1)
            dve.wait_ge(x_projected, TILES)
            for t in range(TILES):
                link(nc.vector.bn_stats(x_stats[:, t, :], ps_p[0][:, t * E:(t + 1) * E]))
                nc.vector.bn_aggr(x_mv[:, t, :], x_stats[:, t, :]).then_inc(x_stats_ready, 1)
            for t in range(TILES):
                dve.wait_ge(x_std_ready, t + 1)
                link(nc.vector.reciprocal(x_rstd[:, t:t + 1], x_std[:, t:t + 1]))
                nc.vector.tensor_scalar(x_hat[:, t, :], ps_p[0][:, t * E:(t + 1) * E], x_mv[:, t, 0:1],
                                        x_rstd[:, t:t + 1], ALU.subtract, ALU.mult).then_inc(x_hat_ready, 1)

            def norm_pair(i, t, first):
                n = PAIRS * i + t
                dve.wait_ge(y_std_ready, n + 1)
                nc.vector.reciprocal(y_rstd[:, 2 * t:2 * t + 2], y_std[:, 2 * t:2 * t + 2]
                                     ).then_inc(y_rstd_ready, 1)
                dve.wait_ge(y_rstd_ready, n + 1)
                if not first:
                    dve.wait_ge(bank_projected, BANKS * (i - 1) + max(
                        k for k in range(BANKS) if bank_pieces(k)[0][0] <= 2 * t + 1) + 1)
                for r in range(2):
                    c = 2 * t + r
                    nc.vector.scalar_tensor_tensor(out=y_norm[:, c, :], in0=ps_y[t % 2][:, r, :],
                                                   scalar=y_rstd[:, c:c + 1], in1=gs_sb[:],
                                                   op0=ALU.mult, op1=ALU.mult).then_inc(y_normed, 1)

            def sum_bank(i, k, first):
                m = BANKS * i + k
                dve.wait_ge(bank_squared, m + 1)
                if not first:
                    dve.wait_ge(p_std_ready, m - BANKS + 1)
                nc.vector.tensor_reduce(p_var[:, k, :],
                                        proj_sq[:, k % 2, :].rearrange("p (s q) -> p s q", q=PR),
                                        AX.X, ALU.add).then_inc(p_var_ready, 1)

            def norm_bank(i, k):
                m = BANKS * i + k
                dve.wait_ge(p_std_ready, m + 1)
                nc.vector.reciprocal(p_rstd[:, k, :], p_std[:, k, :]).then_inc(p_rstd_ready, 1)
                dve.wait_ge(p_rstd_ready, m + 1)
                nc.vector.tensor_tensor(
                    p_hat[:, k * SPB:(k + 1) * SPB, :], ps_p[k % 2][:].rearrange("p (s q) -> p s q", q=PR),
                    p_rstd[:, k, :].rearrange("p (s q) -> p s q", q=1).broadcast_to([P, SPB, PR]),
                    ALU.mult).then_inc(p_hat_ready, 1)

            def make_items(i, first):
                dve.wait_ge(p_hat_ready, BANKS * (i + 1))
                if not first:
                    dve.wait_ge(z_ready, ZSTEPS * i)
                for q in range(PR):
                    nc.vector.tensor_scalar(items[:, :, q], p_hat[:, :, q], gsi_sb[:, q:q + 1],
                                            bsi_sb[:, q:q + 1], ALU.mult, ALU.add)
                nc.vector.tensor_copy(items[:, :, PR],
                                      x_t[:, bass.ds(i, 1)].rearrange("p a g j -> p (a g j)")
                                      ).then_inc(items_ready, 1)

            def copy_z(i, s, first):
                dve.wait_ge(z_ready, ZSTEPS * i + s + 1)
                if not first:
                    dve.wait_ge(z_regrouped, 16 * J * QA * i)
                z = ps_z[:, 0:GZ * NI].rearrange("p (g q) -> p g q", q=NI)
                full = (QA - 1) * QB
                nc.vector.tensor_copy(z_jp[:, 0:QA - 1, s * GZ:(s + 1) * GZ, :],
                                      z[:, :, 0:full].rearrange("p g (a b) -> p a g b", b=QB))
                nc.vector.tensor_copy(z_jp[:, QA - 1, s * GZ:(s + 1) * GZ, 0:NI - full],
                                      z[:, :, full:NI]).then_inc(z_copied, 1)

            def norm_out(i):
                dve.wait_ge(o_ready, i + 1)
                nc.vector.bn_stats(o_stats[:], ps_m[:]).then_inc(o_stats_ready, 1)
                counted = i + 1 if isinstance(i, int) else dve.snap(i + 1)
                dve.wait_ge(o_stats_ready, 1)
                dve.wait_ge(o_stats_ready, counted)
                nc.vector.bn_aggr(o_mv[:], o_stats[:]).then_inc(o_mv_ready, 1)
                dve.wait_ge(o_std_ready, i + 1)
                nc.vector.reciprocal(o_rstd[:], o_std[:]).then_inc(o_rstd_ready, 1)
                dve.wait_ge(o_rstd_ready, i + 1)
                nc.vector.tensor_scalar(o_hat[:], ps_m[:, 0:USED], o_mv[:, 0:1], o_rstd[:, 0:1],
                                        ALU.subtract, ALU.mult).then_inc(o_hat_ready, 1)

            def renew_index(i, half):
                lo, hi = HALVES[half]
                dve.wait_ge(pair_turned, PAIRS * i + hi)
                nc.vector.tensor_copy(tile_index[:, 2 * lo:2 * hi],
                                      row_index[:, bass.ds((i + 1) * CH + 2 * lo, 2 * (hi - lo))]
                                      ).then_inc(index_ready, 1)

            def front_step(i, t, first):
                for half, (lo, hi) in enumerate(HALVES):
                    if t == hi + 1:
                        renew_index(i, half)
                if 2 <= t <= PAIRS + 1:
                    norm_pair(i, t - 2, first)
                for k in range(BANKS):
                    if pair_of_bank(k) == t - 3:
                        sum_bank(i, k, first)
                    if pair_of_bank(k) == t - 4:
                        norm_bank(i, k)

            def back_step(i, t, first):
                if 5 <= t < 5 + ZSTEPS:
                    copy_z(i, t - 5, first)
                if t == 11:
                    norm_out(i)

            for t in range(PAIRS + 4):
                front_step(0, t, True)
            dve.wait_ge(x_ready, TILES)
            make_items(0, True)
            with dve.Fori(1, TILES) as i:
                for t in range(PAIRS + 4):
                    front_step(i, t, False)
                    back_step(i - 1, t, False)
                make_items(i, False)
            for t in range(PAIRS + 4):
                back_step(TILES - 1, t, False)

        @block.tensor
        def _(pe):
            pe.wait_ge(weights_ready, 1)
            nc.tensor.matmul(ps_m[0:PARTS * PARTS, 0:PR], ones_sb[:], wsit_c[:],
                             start=True, stop=True).then_inc(sc_summed, 1)
            pe.wait_ge(x_loaded, 32)
            for t in range(TILES):
                for c in range(DK):
                    mm = nc.tensor.matmul(ps_p[0][:, t * E:(t + 1) * E], dense_sb[:, c, t * P:(t + 1) * P],
                                          wd_sb[:, c, :], start=(c == 0), stop=(c == DK - 1))
                mm.then_inc(x_projected, 1)
            for t in range(TILES):
                pe.wait_ge(x_hat_ready, t + 1)
                nc.tensor.transpose(ps_z[:, t * P:(t + 1) * P], x_hat[:, t, :], eye_sb[:]
                                    ).then_inc(x_turned, 1)
            pe.wait_ge(weights_ready, 2)

            def turn_pair(i, t, first):
                n = PAIRS * i + t
                for c in (2 * t, 2 * t + 1):
                    pe.wait_ge(gathered[c], 16 * (i + 1))
                if t >= 2 or not first:
                    pe.wait_ge(pair_copied, n if t == 0 else n - 1)
                nc.tensor.transpose(ps_t[t % 2][:], emb[:, 2 * t:2 * t + 2, :].rearrange("p a b -> p (a b)"),
                                    eye_sb[:]).then_inc(pair_turned, 1)

            def embed_pair(i, t, first):
                n = PAIRS * i + t
                pe.wait_ge(pair_copied, n + 1)
                if t >= 2 or not first:
                    pe.wait_ge(y_normed, 2 * (n if t == 0 else n - 1))
                nc.tensor.matmul(ps_y[t % 2][:], emb_t[:, t, :], ws_c[:], start=True, stop=True
                                 ).then_inc(pair_embedded, 1)

            def project_bank(i, k, first):
                m = BANKS * i + k
                pe.wait_ge(y_normed, CH * i + bank_pieces(k)[-1][0] + 1)
                if k >= 2 or not first:
                    pe.wait_ge(p_hat_ready, m - 1)
                out = ps_p[k % 2][:].rearrange("p (s q) -> p s q", q=PR)
                nc.tensor.matmul(out, bs_parts[:], sc_parts[:].rearrange("p (s q) -> p s q", s=1).broadcast_to(
                    [PARTS * PARTS, SPB, PR]), start=True, stop=True, skip_group_check=True)
                pieces = bank_pieces(k)
                for c, b0, o0, nb in pieces:
                    mm = nc.tensor.matmul(out[:, o0:o0 + nb, :], y_norm[:, c, :],
                                          wsi_c[:, SPC * (c % PERIOD) + b0:SPC * (c % PERIOD) + b0 + nb, :],
                                          start=False, stop=True, skip_group_check=True)
                mm.then_inc(bank_projected, 1)

            def z_step(i, s):
                if s == 0:
                    pe.wait_ge(items_ready, i + 1)
                else:
                    pe.wait_ge(z_copied, ZSTEPS * i + s)
                for g in range(GZ):
                    for j in range(J):
                        b = J * (s * GZ + g) + j
                        mm = nc.tensor.matmul(ps_z[PR * j:PR * j + PR, g * NI:(g + 1) * NI],
                                              items[:, b, 0:PR], items[:, b, :], start=True, stop=True)
                mm.then_inc(z_ready, 1)

            def interact(i, first):
                pe.wait_ge(z_regrouped, 16 * J * QA * (i + 1))
                if not first:
                    pe.wait_ge(y_copied, i)
                for q in range(QB):
                    mm = nc.tensor.matmul(ps_m[:], z_qp[:, :, :, q].rearrange("p j g -> p (j g)"), wl_sb[:, q, :],
                                          start=(q == 0), stop=(q == QB - 1))
                mm.then_inc(o_ready, 1)

            def turn_out(i):
                pe.wait_ge(o_hat_ready, i + 1)
                for c in range(ZK):
                    mm = nc.tensor.transpose(ps_m[:, c * P:(c + 1) * P], o_hat[:, c * P:(c + 1) * P], eye_sb[:])
                mm.then_inc(o_turned, 1)

            def layer_1(i):
                pe.wait_ge(z_t_ready, ZK * (i + 1))
                for m in range(HK):
                    for c in range(ZK + DK):
                        rhs = z_t[:, c, :] if c < ZK else dense_sb[:, c - ZK, bass.ds(i * P, P)]
                        mm = nc.tensor.matmul(ps_m[:, m * P:(m + 1) * P], w1_sb[:, c, m * P:(m + 1) * P], rhs,
                                              start=(c == 0), stop=(c == ZK + DK - 1))
                mm.then_inc(h1_summed, 1)

            def layer_2(i):
                pe.wait_ge(h1_ready, HK * (i + 1))
                for m in range(H2 // P):
                    for c in range(HK):
                        mm = nc.tensor.matmul(ps_m[:, m * P:(m + 1) * P], w2_sb[:, c, m * P:(m + 1) * P],
                                              h1_t[:, c, :], start=(c == 0), stop=(c == HK - 1))
                mm.then_inc(h2_summed, 1)

            def layer_3(i):
                pe.wait_ge(h2_ready, H2 // P * (i + 1))
                for c in range(H2 // P):
                    mm = nc.tensor.matmul(ps_m[0:1, 0:P], w3_sb[:, c:c + 1], h2_t[:, c, :],
                                          start=(c == 0), stop=(c == H2 // P - 1))
                mm.then_inc(y_summed, 1)

            def front_step(i, t, first):
                if t < PAIRS:
                    turn_pair(i, t, first)
                if 1 <= t <= PAIRS:
                    embed_pair(i, t - 1, first)
                for k in range(BANKS):
                    if pair_of_bank(k) == t - 3:
                        project_bank(i, k, first)

            def back_step(i, t, first):
                if 5 <= t < 5 + ZSTEPS:
                    z_step(i, t - 5)
                if t == 10:
                    pe.wait_ge(wl_loaded, 16)
                    interact(i, first)
                if t == 11:
                    turn_out(i)
                if t == 12:
                    pe.wait_ge(top_loaded, 16 * TOP)
                    layer_1(i)
                if t == 13:
                    layer_2(i)
                if t == 14:
                    layer_3(i)

            pe.wait_ge(x_ready, TILES)
            for t in range(PAIRS + 4):
                front_step(0, t, True)
            with pe.Fori(1, TILES) as i:
                for t in range(PAIRS + 4):
                    front_step(i, t, False)
                    back_step(i - 1, t, False)
            for t in range(PAIRS + 4):
                back_step(TILES - 1, t, False)


def kernel(**inputs):
    import concourse.bacc as bacc
    from concourse.bass_utils import run_bass_kernel_spmd

    a = {k: np.asarray(v) for k, v in inputs.items()}
    arrays = {}

    base = np.concatenate([[0], np.cumsum(VOCAB)[:-1]]).astype(np.int32)
    arrays["rows_at"] = np.ascontiguousarray(a["ids"].reshape(TILES * CH, P).T)
    arrays["table_base"] = np.ascontiguousarray(np.tile(base, B).reshape(TILES * CH, P).T)
    arrays["tables"] = np.concatenate([a[f"tbl_{t}"] for t in range(NT)], axis=0)

    dense = a["r_dense_t"].T.reshape(DK, P, TILES, G, J).transpose(1, 0, 2, 4, 3)
    arrays["dense"] = np.ascontiguousarray(dense).reshape(P, DK, B)

    def k_major(w, k):
        return np.ascontiguousarray(w.reshape(k, P, -1).transpose(1, 0, 2))

    arrays["wd"] = k_major(a["L0_rec_Wd"].T, DK)
    arrays["gd"] = a["L0_rec_gd"].reshape(P, 1)
    arrays["bd"] = a["L0_rec_bd"].reshape(P, 1)
    arrays["ws"] = np.zeros((2, D, 2, E), np.float32)
    for r in range(2):
        arrays["ws"][r, :, r] = a["L0_rec_Ws"].T
    arrays["ws"] = arrays["ws"].reshape(P, 2, E)
    arrays["gs"] = a["L0_rec_gs"]
    arrays["bs"] = a["L0_rec_bs"]

    wsi_t = np.ascontiguousarray(a["L0_rec_Wsi"].T)
    blocks = np.zeros((P, PERIOD, SPC, PR), np.float32)
    for c in range(PERIOD):
        for r in range(P):
            sample, table = divmod(P * c + r, NT)
            blocks[r, c, sample - chunk_samples(c)[0]] = wsi_t[table]
    arrays["wsi_blocks"] = blocks.reshape(P, -1)
    arrays["wsi_t"] = wsi_t
    arrays["gsi"] = a["L0_rec_gsi"]
    arrays["bsi"] = a["L0_rec_bsi"]

    wl_t = a["L0_rec_Wl"].T
    slots = np.zeros((QA * QB, PR, MD), np.float32)
    for n, (hi, lo) in enumerate(zip(*np.tril_indices(NI, k=-1))):
        slots[lo - 1 if lo else PR, hi - 1] = wl_t[n]
    slots = slots.reshape(QA, QB, PR, MD).transpose(0, 2, 1, 3)
    arrays["wl_slots"] = np.ascontiguousarray(slots).reshape(P, QB, MD)
    arrays["gl"] = np.ascontiguousarray(a["L0_rec_gl"][:USED].reshape(ZK, P).T)
    arrays["bl"] = np.ascontiguousarray(a["L0_rec_bl"][:USED].reshape(ZK, P).T)

    w1 = a["W_top1"]
    arrays["w1"] = k_major(np.concatenate([w1[:USED], w1[MD:]], axis=0), ZK + DK)
    arrays["b1"] = np.ascontiguousarray(a["b_top1"].reshape(HK, P).T)
    arrays["w2"] = k_major(a["W_top2"], HK)
    arrays["b2"] = np.ascontiguousarray(a["b_top2"].reshape(H2 // P, P).T)
    arrays["w3"] = np.ascontiguousarray(a["W_top3"].reshape(H2 // P, P, 1))

    arrays["eye"] = np.eye(P, dtype=np.float32)
    masks = np.zeros((PARTS * PARTS, 2 * PARTS), np.float32)
    for r in range(PARTS * PARTS):
        masks[r, r // PARTS] = 1
        masks[r, PARTS + r % PARTS] = 1
    arrays["part_masks"] = masks

    nc = bacc.Bacc("TRN2", target_bir_lowering=False, num_devices=1)
    args = [nc.dram_tensor(f"in_{k}", v.shape, mybir.dt.from_np(v.dtype), kind="ExternalInput").ap()
            for k, v in arrays.items()]
    y_out = nc.dram_tensor("y_out", (1, B), F32, kind="ExternalOutput").ap()
    build(nc, *args, y_out)
    r = run_bass_kernel_spmd(nc, [{f"in_{k}": v for k, v in arrays.items()}], core_ids=[0])
    return r.results[0]["y_out"].reshape(B, 1)
```

```python
from contextlib import ExitStack

import numpy as np

import concourse.bass as bass
from concourse import mybir

ALU = mybir.AluOpType
ACT = mybir.ActivationFunctionType
AX = mybir.AxisListType
F32 = mybir.dt.float32
BF16 = mybir.dt.bfloat16
I32 = mybir.dt.int32

P = 128
EPS = 1e-5
B = 512
NT = 26
D = 64
E = 128
PR = 32
NI = PR + 1
DD = 256
MD = 512
USED = 384
H1, H2 = 512, 256
TILES = B // P
CH = NT * P // P
PAIRS = CH // 2
PERIOD = CH // 2
SPC = 6
SPB = 512 // PR
BANKS = P // SPB
J, G = 4, P // 4
IW = PR + 2
NZ = IW - 1
QA, QB = 4, 9
SUM_SLOT = divmod(1, QB)
DENSE_SUM_SLOT = divmod(NZ, QB)
CONST_SLOT = divmod(NZ + 1, QB)
GZ = 8
ZSTEPS = G // GZ
PARTS = 3
LAG_TURN, LAG_EMBED, LAG_PROJECT, LAG_SUM_BANK, LAG_NORM_BANK, LAG_Z, LAG_COPY_Z = 0, 1, 3, 4, 5, 6, 7
LAG_INTERACT, LAG_NORM_OUT, LAG_TURN_OUT = (8, 9), 9, 10
LAG_LAYER_1, LAG_LAYER_2 = (11, 12), 13
DENSE_AT = (1, 3, 5)
FOLD_AT = 6
DK, HK, ZK = DD // P, H1 // P, USED // P
CONSTS = {"ws": 2 * E, "gs": E, "wsi_t": PR, "part_masks": 2 * PARTS, "bs": E, "eye": P, "gd": 1, "bd": 1,
          "gsi_p": 1, "gsi_q": QB, "bsi_col": P, "gl": ZK, "bl": ZK, "b1": HK, "b2": H2 // P, "w3": H2 // P}
VOCAB = [1250, 1000, 12500, 1000, 1250, 125000, 1000, 1000, 1250, 1250, 125000, 1250, 1250,
         125000, 12500, 12500, 1000, 12500, 1000, 1000, 12500, 1000, 12500, 12500, 1250, 1250]


def chunk_samples(c):
    return P * c // NT, (P * c + P - 1) // NT


def bank_pieces(k):
    half, kb = divmod(k, BANKS // 2)
    pieces = []
    for c in range(PERIOD):
        s0, s1 = chunk_samples(c)
        a, b = max(s0, SPB * kb), min(s1, SPB * kb + SPB - 1)
        if a <= b:
            pieces.append((half * PERIOD + c, a - s0, a - SPB * kb, b - a + 1))
    return pieces


def bank_after(u):
    return [k for k in range(BANKS) if bank_pieces(k)[-1][0] // 2 == u]


def z_after(u):
    return [k // 2 for k in bank_after(u) if k % 2]


def lagged(i, t, lag, own, before):
    if t >= lag:
        return [(i, t - lag)] if own else []
    return [(i - 1, t - lag + PAIRS)] if before else []


def behind(tile, n, depth):
    return not (isinstance(tile, int) and n < depth)


def build(nc, rows_at, tables, consts, wsi_blocks, dense, wl_slots, bsi_fold, w1, w2, y_out):
    with ExitStack() as ctx:
        def sb(name, shape, dt=F32):
            return ctx.enter_context(nc.sbuf_tensor(name, shape, dt))

        def psum(name, shape):
            return ctx.enter_context(nc.psum_tensor(name, shape, F32))

        def sem(name):
            return ctx.enter_context(nc.semaphore(name))

        consts_sb = sb("consts_sb", [P, sum(CONSTS.values())])

        def const(name, rows=P):
            names = list(CONSTS)
            at = sum(CONSTS[k] for k in names[:names.index(name)])
            return consts_sb[0:rows, at:at + CONSTS[name]]

        eye_sb = const("eye")
        ws_raw = const("ws").rearrange("p (r e) -> p r e", r=2)
        gs_sb, bs_sb = const("gs"), const("bs", PARTS * PARTS)
        wsit_raw, masks_sb = const("wsi_t", NT), const("part_masks", PARTS * PARTS)
        gd_sb, bd_sb, gl_sb, bl_sb = const("gd"), const("bd"), const("gl"), const("bl")
        gsi_p_sb, gsi_q_sb = const("gsi_p"), const("gsi_q")
        bsi_col_sb = const("bsi_col", PR)
        b1_sb, b2_sb, w3_sb = const("b1"), const("b2"), const("w3")
        rows_sb = sb("rows_sb", [P, 2, TILES * CH], I32)
        row_index = sb("row_index", [P, (TILES + 1) * CH], I32)
        tile_index = sb("tile_index", [P, CH], I32)
        ws_mean = sb("ws_mean", [P, 2])
        ws_c = sb("ws_c", [P, 2, E])
        wsi_raw = sb("wsi_raw", [P, PERIOD * SPC, PR])
        wsi_mean = sb("wsi_mean", [P, PERIOD * SPC])
        wsi_c = sb("wsi_c", [P, PERIOD * SPC, PR])
        wsit_mean = sb("wsit_mean", [NT, 1])
        wsit_c = sb("wsit_c", [NT, PR])
        ones_sb = sb("ones_sb", [NT, PARTS * PARTS])
        sc_sb = sb("sc_sb", [PARTS * PARTS, PR])
        bs_parts = sb("bs_parts", [PARTS * PARTS, E], BF16)
        sc_parts = sb("sc_parts", [PARTS * PARTS, PR], BF16)
        split_hi = sb("split_hi", [PARTS * PARTS, 2, PARTS, E], BF16)
        split_f = sb("split_f", [PARTS * PARTS, 2, 4, E])
        gsi_pq = sb("gsi_pq", [P, QB])
        bsi_fold_sb = sb("bsi_fold_sb", [P, QB, P])
        sum_raw = sb("sum_raw", [PR, MD])
        ones_e = sb("ones_e", [P, PR])
        dense_sum = sb("dense_sum", [P, TILES, J, G])
        wl_sb = sb("wl_sb", [P, QB, MD])
        w1_sb = sb("w1_sb", [P, ZK + DK, H1])
        w2_sb = sb("w2_sb", [P, HK, H2])
        eps_sb = sb("eps_sb", [P, 1])
        dense_wd = sb("dense_wd", [P, DK, B + E])
        dense_sb, wd_sb = dense_wd[:, :, 0:B], dense_wd[:, :, B:B + E]
        x_stats = sb("x_stats", [P, TILES, 6])
        x_mv = sb("x_mv", [P, TILES, 2])
        x_std = sb("x_std", [P, TILES])
        x_rstd = sb("x_rstd", [P, TILES])
        x_hat = sb("x_hat", [P, TILES, E])
        x_t = sb("x_t", [P, TILES, G, J])
        emb = sb("emb", [P, CH, D])
        emb_t = sb("emb_t", [P, PAIRS, P])
        sq_junk = sb("sq_junk", [P, 2, E])
        y_var = sb("y_var", [P, CH])
        y_std = sb("y_std", [P, CH])
        y_rstd = sb("y_rstd", [P, CH])
        y_norm = sb("y_norm", [P, CH, E])
        proj_sq = sb("proj_sq", [P, 2, SPB * PR])
        p_var = sb("p_var", [P, BANKS, SPB])
        p_std = sb("p_std", [P, BANKS, SPB])
        p_rstd = sb("p_rstd", [P, BANKS, SPB])
        items = sb("items", [P, P, IW])
        z_jp = sb("z_jp", [P, QA, G, QB])
        z_qp = sb("z_qp", [P, J, G, QB])
        o_stats = sb("o_stats", [P, 6])
        o_mv = sb("o_mv", [P, 2])
        o_std = sb("o_std", [P, 1])
        o_rstd = sb("o_rstd", [P, 1])
        o_hat = sb("o_hat", [P, USED])
        z_t = sb("z_t", [P, ZK, P])
        h1_t = sb("h1_t", [P, HK, P])
        h2_t = sb("h2_t", [P, H2 // P, P])
        y_sb = sb("y_sb", [1, TILES, G, J])

        ps_t = [psum(f"ps_t{r}", [P, P]) for r in range(2)]
        ps_y = [psum(f"ps_y{r}", [P, 2, E]) for r in range(2)]
        ps_p = [psum(f"ps_p{r}", [P, SPB * PR]) for r in range(2)]
        ps_z = psum("ps_z", [P, 512])
        ps_m = psum("ps_m", [P, 512])

        rows_loaded = sem("rows_loaded")
        consts_loaded = sem("consts_loaded")
        wsi_loaded = sem("wsi_loaded")
        x_loaded = sem("x_loaded")
        wl_loaded = sem("wl_loaded")
        top_loaded = sem("top_loaded")
        index_ready = sem("index_ready")
        dve_prep = sem("dve_prep")
        weights_ready = sem("weights_ready")
        sc_summed = sem("sc_summed")
        x_projected = sem("x_projected")
        x_std_ready = sem("x_std_ready")
        x_stats_ready = sem("x_stats_ready")
        x_hat_ready = sem("x_hat_ready")
        x_counted = sem("x_counted")
        x_rstd_ready = sem("x_rstd_ready")
        x_turned = sem("x_turned")
        x_ready = sem("x_ready")
        gathered = [sem(f"gathered{c}") for c in range(CH)]
        pair_turned = sem("pair_turned")
        pair_copied = sem("pair_copied")
        pair_embedded = sem("pair_embedded")
        y_squared = sem("y_squared")
        y_std_ready = sem("y_std_ready")
        y_rstd_ready = sem("y_rstd_ready")
        y_normed = sem("y_normed")
        bank_projected = sem("bank_projected")
        bank_squared = sem("bank_squared")
        p_var_ready = sem("p_var_ready")
        p_std_ready = sem("p_std_ready")
        p_rstd_ready = sem("p_rstd_ready")
        p_hat_ready = sem("p_hat_ready")
        dense_summed = sem("dense_summed")
        sums_folded = sem("sums_folded")
        const_folded = sem("const_folded")
        sum_raw_ready = sem("sum_raw_ready")
        wl_ready = sem("wl_ready")
        z_ready = sem("z_ready")
        z_copied = sem("z_copied")
        z_moved = sem("z_moved")
        wl_scaled = sem("wl_scaled")
        sums_taken = sem("sums_taken")
        x_summed = sem("x_summed")
        z_regrouped = sem("z_regrouped")
        m_free = sem("m_free")
        o_ready = sem("o_ready")
        o_stats_ready = sem("o_stats_ready")
        o_mv_ready = sem("o_mv_ready")
        o_std_ready = sem("o_std_ready")
        o_rstd_ready = sem("o_rstd_ready")
        o_hat_ready = sem("o_hat_ready")
        o_turned = sem("o_turned")
        z_t_ready = sem("z_t_ready")
        h1_summed = sem("h1_summed")
        h1_ready = sem("h1_ready")
        h2_summed = sem("h2_summed")
        h2_ready = sem("h2_ready")
        y_summed = sem("y_summed")
        y_stored = sem("y_stored")

        DS_ROWS = slice(PR * DENSE_SUM_SLOT[0], PR * DENSE_SUM_SLOT[0] + PR)
        HALVES = ((0, 7), (7, PAIRS))
        block = ctx.enter_context(nc.Block())

        @block.sync
        def _(sp):
            sp.dma_start(rows_sb[:], rows_at).then_inc(rows_loaded, 16)
            sp.dma_start(consts_sb[:], consts).then_inc(consts_loaded, 16)
            sp.dma_start(wsi_raw[:].rearrange("p a b -> p (a b)"), wsi_blocks).then_inc(wsi_loaded, 16)
            sp.dma_start(dense_wd[:], dense).then_inc(x_loaded, 16)
            sp.wait_ge(pair_turned, 2)
            sp.dma_start(wl_sb[:], wl_slots).then_inc(wl_loaded, 16)
            sp.dma_start(bsi_fold_sb[:], bsi_fold).then_inc(wl_loaded, 16)
            sp.dma_start(w1_sb[:], w1).then_inc(top_loaded, 16)
            sp.dma_start(w2_sb[:], w2).then_inc(top_loaded, 16)
            sp.wait_ge(m_free, TILES + 1)
            sp.dma_start(y_out, y_sb[:].rearrange("p a b c -> p (a b c)")).then_inc(y_stored, 16)
            sp.wait_ge(y_stored, 16)

        @block.gpsimd
        def _(pool):
            halves = pool.alloc_register("halves")
            pool.reg_mov(halves, 1)

            def gather():
                for c in range(CH):
                    for half, (lo, hi) in enumerate(HALVES):
                        if c == 2 * lo:
                            pool.wait_ge(index_ready, halves)
                            pool.reg_add(halves, halves, 1)
                    pool.indirect_dma_start(
                        out=emb[:, c, :], out_offset=None, in_=tables,
                        in_offset=bass.IndirectOffsetOnAxis(
                            ap=tile_index[:, c:c + 1], axis=0),
                    ).then_inc(gathered[c], 16)

            with pool.Fori(0, TILES):
                gather()

        @block.scalar
        def _(act):
            def std_dense():
                act.wait_ge(x_stats_ready, TILES)
                nc.scalar.activation(x_std[:].rearrange("p (t a) -> p t a", a=1), x_mv[:, :, 1:2], ACT.Sqrt,
                                     bias=eps_sb[:, 0:1]).then_inc(x_std_ready, 1)

            def scale_dense():
                act.wait_ge(x_turned, 1)
                for t in range(TILES):
                    nc.scalar.activation(x_t[:, t].rearrange("p g j -> p j g"),
                                         ps_z[:, t * P:(t + 1) * P].rearrange("p (j g) -> p j g", j=J),
                                         ACT.Identity, bias=bd_sb[:, 0:1], scale=gd_sb[:, 0:1]
                                         ).then_inc(x_ready, 1)

            def copy_pair(i, t):
                n = PAIRS * i + t
                act.wait_ge(pair_turned, n + 1)
                if behind(i, t, 4):
                    act.wait_ge(pair_embedded, n - 3)
                nc.scalar.copy(emb_t[:, t, :], ps_t[t % 2][:]).then_inc(pair_copied, 1)

            def square_pair(i, t):
                n = PAIRS * i + t
                act.wait_ge(pair_embedded, n + 1)
                for r in range(2):
                    nc.scalar.activation(sq_junk[:, r, :], ps_y[t % 2][:, r, :], ACT.Square,
                                         scale=float(E) ** -0.5,
                                         accum_out=y_var[:, 2 * t + r:2 * t + r + 1]
                                         ).then_inc(y_squared, 1)
                act.wait_ge(y_squared, 2 * n + 2)
                if behind(i, t, 4):
                    act.wait_ge(y_rstd_ready, n - 3)
                nc.scalar.activation(y_std[:, 2 * t:2 * t + 2], y_var[:, 2 * t:2 * t + 2], ACT.Sqrt,
                                     bias=eps_sb[:, 0:1]).then_inc(y_std_ready, 1)

            def square_bank(i, k):
                m = BANKS * i + k
                act.wait_ge(bank_projected, m + 1)
                if behind(i, k, 2):
                    act.wait_ge(p_var_ready, m - 1)
                nc.scalar.activation(proj_sq[:, k % 2, :], ps_p[k % 2][:], ACT.Square,
                                     scale=float(PR) ** -0.5).then_inc(bank_squared, 1)

            def std_bank(i, k):
                m = BANKS * i + k
                act.wait_ge(p_var_ready, m + 1)
                if behind(i, k, 4):
                    act.wait_ge(p_rstd_ready, m - 3)
                nc.scalar.activation(p_std[:, k, :], p_var[:, k, :], ACT.Sqrt,
                                     bias=eps_sb[:, 0:1]).then_inc(p_std_ready, 1)

            def std_out(i):
                act.wait_ge(o_mv_ready, i + 1)
                nc.scalar.activation(o_std[:], o_mv[:, 1:2], ACT.Sqrt,
                                     bias=eps_sb[:, 0:1]).then_inc(o_std_ready, 1)

            def scale_z(i):
                act.wait_ge(o_turned, i + 1)
                for c in range(ZK):
                    nc.scalar.activation(z_t[:, c, :], ps_m[:, c * P:(c + 1) * P], ACT.Identity,
                                         bias=bl_sb[:, c:c + 1], scale=gl_sb[:, c:c + 1]
                                         ).then_inc(z_t_ready, 1)

            def relu_1(i):
                act.wait_ge(h1_summed, i + 1)
                for c in range(HK):
                    nc.scalar.activation(h1_t[:, c, :], ps_m[:, c * P:(c + 1) * P], ACT.Relu,
                                         bias=b1_sb[:, c:c + 1]).then_inc(h1_ready, 1)

            def relu_2(i):
                act.wait_ge(h2_summed, i + 1)
                for c in range(H2 // P):
                    nc.scalar.activation(h2_t[:, c, :], ps_m[:, c * P:(c + 1) * P], ACT.Relu,
                                         bias=b2_sb[:, c:c + 1]).then_inc(h2_ready, 1)

            def copy_y(i):
                act.wait_ge(y_summed, i + 1)
                nc.scalar.copy(y_sb[0:1, bass.ds(i, 1)].rearrange("p a g j -> p a j g"),
                               ps_m[0:1, 0:P].rearrange("p (a j g) -> p a j g", a=1, j=J)
                               ).then_inc(m_free, 1)

            def step(i, t, own, before):
                for tile, u in lagged(i, t, LAG_TURN, own, before):
                    copy_pair(tile, u)
                for tile, u in lagged(i, t, LAG_EMBED, own, before):
                    square_pair(tile, u)
                for tile, u in lagged(i, t, LAG_NORM_BANK, own, before):
                    for k in bank_after(u):
                        std_bank(tile, k)
                for tile, u in lagged(i, t, LAG_SUM_BANK, own, before):
                    for k in bank_after(u):
                        square_bank(tile, k)
                for lag, work in ((LAG_NORM_OUT, std_out), (LAG_TURN_OUT, scale_z), (LAG_LAYER_1[-1], relu_1),
                                  (LAG_LAYER_2, relu_2), (LAG_LAYER_2, copy_y)):
                    for tile, u in lagged(i, t, lag, own, before):
                        if u == PAIRS - 1:
                            work(tile)

            act.wait_ge(weights_ready, 1)
            for t in range(PAIRS):
                step(0, t, True, False)
                if t == DENSE_AT[0]:
                    std_dense()
                if t == DENSE_AT[1]:
                    scale_dense()
            with act.Fori(1, TILES) as i:
                for t in range(PAIRS):
                    step(i, t, True, True)
            for t in range(PAIRS):
                step(TILES, t, False, True)

        @block.vector
        def _(dve):
            chain = [0]

            def link(ins):
                chain[0] += 1
                ins.then_inc(dve_prep, 1)
                dve.wait_ge(dve_prep, chain[0])

            dve.wait_ge(rows_loaded, 16)
            nc.vector.memset(row_index[:, TILES * CH:], 0)
            link(nc.vector.tensor_tensor(row_index[:, 0:TILES * CH], rows_sb[:, 0, :], rows_sb[:, 1, :], ALU.add))
            nc.vector.tensor_copy(tile_index[:], row_index[:, 0:CH]).then_inc(index_ready, len(HALVES))
            nc.vector.memset(z_jp[:, QA - 1, :, NZ - (QA - 1) * QB:QB], 1.0)
            nc.vector.memset(items[:, :, 1], 1.0)
            nc.vector.memset(ones_e[:], 1.0)
            nc.vector.memset(ones_sb[:], 1.0)
            link(nc.vector.memset(eps_sb[:], EPS))
            dve.wait_ge(consts_loaded, 16)
            link(nc.vector.tensor_reduce(ws_mean[:], ws_raw[:], AX.X, ALU.add))
            link(nc.vector.tensor_scalar(ws_mean[:], ws_mean[:], 1.0 / E, None, ALU.mult))
            link(nc.vector.tensor_tensor(ws_c[:], ws_raw[:],
                                         ws_mean[:].rearrange("p (a b) -> p a b", b=1).broadcast_to([P, 2, E]),
                                         ALU.subtract))
            link(nc.vector.tensor_reduce(wsit_mean[:], wsit_raw[:], AX.X, ALU.add))
            link(nc.vector.tensor_scalar(wsit_mean[:], wsit_mean[:], 1.0 / PR, None, ALU.mult))
            link(nc.vector.tensor_scalar(wsit_c[:], wsit_raw[:], wsit_mean[:, 0:1], None, ALU.subtract))
            nc.vector.tensor_copy(wsit_mean[:], wsit_mean[:]).then_inc(weights_ready, 1)
            dve.wait_ge(wsi_loaded, 16)
            link(nc.vector.tensor_reduce(wsi_mean[:], wsi_raw[:], AX.X, ALU.add))
            link(nc.vector.tensor_scalar(wsi_mean[:], wsi_mean[:], 1.0 / PR, None, ALU.mult))
            link(nc.vector.tensor_tensor(wsi_c[:], wsi_raw[:],
                                         wsi_mean[:].rearrange("p (a b) -> p a b", b=1).broadcast_to(
                                             [P, PERIOD * SPC, PR]), ALU.subtract))
            dve.wait_ge(sc_summed, 1)
            nc.vector.tensor_copy(sc_sb[:], ps_m[0:PARTS * PARTS, 0:PR]).then_inc(m_free, 1)
            dve.wait_ge(m_free, 1)
            for side, (src, dst, n) in enumerate(((bs_sb, bs_parts, E), (sc_sb, sc_parts, PR))):
                rest = src[:, 0:n]
                total = None
                for q in range(PARTS):
                    hi = split_hi[:, side, q, 0:n]
                    link(nc.vector.tensor_copy(hi, rest))
                    if q < PARTS - 1:
                        link(nc.vector.tensor_tensor(split_f[:, side, q, 0:n], rest, hi, ALU.subtract))
                        rest = split_f[:, side, q, 0:n]
                    mask = masks_sb[:, PARTS * side + q:PARTS * side + q + 1]
                    into = dst[:, 0:n] if q == PARTS - 1 else split_f[:, side, 2 + q, 0:n]
                    if total is None:
                        link(nc.vector.tensor_scalar(into, hi, mask, None, ALU.mult))
                    else:
                        link(nc.vector.scalar_tensor_tensor(out=into, in0=hi, scalar=mask, in1=total,
                                                            op0=ALU.mult, op1=ALU.add))
                    total = into
            nc.vector.tensor_copy(wsit_mean[:], wsit_mean[:]).then_inc(weights_ready, 1)

            def dense_stats():
                dve.wait_ge(x_projected, 1)
                for t in range(TILES):
                    nc.vector.bn_stats(x_stats[:, t, :], ps_m[:, t * E:(t + 1) * E]).then_inc(x_counted, 1)
                for t in range(TILES):
                    dve.wait_ge(x_counted, t + 1)
                    nc.vector.bn_aggr(x_mv[:, t, :], x_stats[:, t, :]).then_inc(x_stats_ready, 1)

            def dense_norm():
                dve.wait_ge(x_std_ready, 1)
                nc.vector.reciprocal(x_rstd[:], x_std[:]).then_inc(x_rstd_ready, 1)
                dve.wait_ge(x_rstd_ready, 1)
                for t in range(TILES):
                    nc.vector.tensor_scalar(x_hat[:, t, :], ps_m[:, t * E:(t + 1) * E], x_mv[:, t, 0:1],
                                            x_rstd[:, t:t + 1], ALU.subtract, ALU.mult).then_inc(x_hat_ready, 1)

            def sum_dense():
                dve.wait_ge(dense_summed, 1)
                nc.vector.tensor_copy(dense_sum[DS_ROWS].rearrange("p t j g -> p (t j g)"), ps_z[DS_ROWS]
                                      ).then_inc(x_summed, 1)
                dve.wait_ge(x_summed, 1)

            def scale_wl(qb):
                if qb == 0:
                    dve.wait_ge(wl_loaded, 32)
                    link(nc.vector.tensor_scalar(gsi_pq[:], gsi_q_sb[:], gsi_p_sb[:, 0:1], None, ALU.mult))
                    link(nc.vector.tensor_scalar(bsi_col_sb[:], bsi_col_sb[:], float(E) / 2, None, ALU.mult))
                    dve.wait_ge(sums_folded, 1)
                    nc.vector.tensor_copy(sum_raw[:], ps_m[0:PR, :]).then_inc(sum_raw_ready, 1)
                nc.vector.tensor_scalar(wl_sb[:, qb, :], wl_sb[:, qb, :], gsi_pq[:, qb:qb + 1], None,
                                        ALU.mult).then_inc(wl_scaled, 1)

            def finish_wl():
                dve.wait_ge(wl_scaled, QB)
                dve.wait_ge(sum_raw_ready, 1)
                (qa, qb) = SUM_SLOT
                nc.vector.tensor_scalar(wl_sb[PR * qa:PR * qa + PR, qb, :], sum_raw[:], gsi_p_sb[0:PR, 0:1],
                                        None, ALU.mult)
                nc.vector.tensor_copy(wl_sb[DS_ROWS, DENSE_SUM_SLOT[1], :], ps_m[DS_ROWS]
                                      ).then_inc(sums_taken, 1)
                dve.wait_ge(const_folded, 1)
                nc.vector.tensor_copy(wl_sb[DS_ROWS, CONST_SLOT[1], :], ps_m[DS_ROWS]).then_inc(wl_ready, 1)

            def norm_pair(i, t):
                n = PAIRS * i + t
                dve.wait_ge(y_std_ready, n + 1)
                nc.vector.reciprocal(y_rstd[:, 2 * t:2 * t + 2], y_std[:, 2 * t:2 * t + 2]
                                     ).then_inc(y_rstd_ready, 1)
                dve.wait_ge(y_rstd_ready, n + 1)
                if t >= 8:
                    dve.wait_ge(bank_projected, BANKS * i + 1)
                elif behind(i, t, PAIRS):
                    reader = max(k for k in range(BANKS) if bank_pieces(k)[0][0] <= 2 * t + 1)
                    dve.wait_ge(bank_projected, BANKS * (i - 1) + reader + 1)
                for r in range(2):
                    c = 2 * t + r
                    nc.vector.scalar_tensor_tensor(out=y_norm[:, c, :], in0=ps_y[t % 2][:, r, :],
                                                   scalar=y_rstd[:, c:c + 1], in1=gs_sb[:],
                                                   op0=ALU.mult, op1=ALU.mult).then_inc(y_normed, 1)

            def sum_bank(i, k):
                m = BANKS * i + k
                dve.wait_ge(bank_squared, m + 1)
                if behind(i, k, 4):
                    dve.wait_ge(p_std_ready, m - 3)
                nc.vector.tensor_reduce(p_var[:, k, :],
                                        proj_sq[:, k % 2, :].rearrange("p (s q) -> p s q", q=PR),
                                        AX.X, ALU.add).then_inc(p_var_ready, 1)

            def norm_bank(i, k):
                m = BANKS * i + k
                dve.wait_ge(p_std_ready, m + 1)
                nc.vector.reciprocal(p_rstd[:, k, :], p_std[:, k, :]).then_inc(p_rstd_ready, 1)
                s = k // 2
                if s >= ZSTEPS // 2:
                    dve.wait_ge(z_ready, ZSTEPS * i + 1)
                elif behind(i, s, ZSTEPS):
                    dve.wait_ge(z_ready, ZSTEPS * (i - 1) + s + 1)
                if k % 2 == 0:
                    nc.vector.tensor_copy(
                        items[:, k * SPB:(k + 2) * SPB, 0],
                        x_t[:, bass.ds(i, 1), s * GZ:(s + 1) * GZ].rearrange("p a g j -> p (a g j)"))
                dve.wait_ge(p_rstd_ready, m + 1)
                nc.vector.tensor_tensor(
                    items[:, k * SPB:(k + 1) * SPB, 2:IW], ps_p[k % 2][:].rearrange("p (s q) -> p s q", q=PR),
                    p_rstd[:, k, :].rearrange("p (s q) -> p s q", q=1).broadcast_to([P, SPB, PR]),
                    ALU.mult).then_inc(p_hat_ready, 1)

            def copy_z(i, s):
                dve.wait_ge(z_ready, ZSTEPS * i + s + 1)
                if s == 0 and behind(i, s, ZSTEPS):
                    dve.wait_ge(z_regrouped, 2 * i)
                z = ps_z[:, 0:GZ * NZ].rearrange("p (g q) -> p g q", q=NZ)
                full = (QA - 1) * QB
                nc.vector.tensor_copy(z_jp[:, 0:QA - 1, s * GZ:(s + 1) * GZ, :],
                                      z[:, :, 0:full].rearrange("p g (a b) -> p a g b", b=QB))
                nc.vector.tensor_copy(z_jp[:, QA - 1, s * GZ:(s + 1) * GZ, 0:NZ - full],
                                      z[:, :, full:NZ]).then_inc(z_copied, 1)

            def regroup_z(i, half):
                groups = slice(half * G // 2, (half + 1) * G // 2)
                dve.wait_ge(z_copied, ZSTEPS * i + ZSTEPS // 2 * (half + 1))
                for j in range(J):
                    for qa in range(QA):
                        nc.vector.tensor_copy(z_qp[PR * qa:PR * qa + PR, j, groups, :],
                                              z_jp[PR * j:PR * j + PR, qa, groups, :]
                                              ).then_inc(z_moved, 1)
                dve.wait_ge(z_moved, J * QA * (2 * i + half + 1))
                nc.vector.tensor_copy(z_qp[DS_ROWS, :, groups, DENSE_SUM_SLOT[1]],
                                      dense_sum[DS_ROWS, bass.ds(i, 1), :, groups].rearrange("p a j g -> p (a j) g")
                                      ).then_inc(z_regrouped, 1)

            def norm_out(i):
                dve.wait_ge(o_ready, i + 1)
                nc.vector.bn_stats(o_stats[:], ps_m[:]).then_inc(o_stats_ready, 1)
                counted = i + 1 if isinstance(i, int) else dve.snap(i + 1)
                dve.wait_ge(o_stats_ready, 1)
                dve.wait_ge(o_stats_ready, counted)
                nc.vector.bn_aggr(o_mv[:], o_stats[:]).then_inc(o_mv_ready, 1)
                dve.wait_ge(o_std_ready, i + 1)
                nc.vector.reciprocal(o_rstd[:], o_std[:]).then_inc(o_rstd_ready, 1)
                dve.wait_ge(o_rstd_ready, i + 1)
                nc.vector.tensor_scalar(o_hat[:], ps_m[:, 0:USED], o_mv[:, 0:1], o_rstd[:, 0:1],
                                        ALU.subtract, ALU.mult).then_inc(o_hat_ready, 1)

            def renew_index(i, half):
                lo, hi = HALVES[half]
                dve.wait_ge(pair_turned, PAIRS * i + hi)
                nc.vector.tensor_copy(tile_index[:, 2 * lo:2 * hi],
                                      row_index[:, bass.ds((i + 1) * CH + 2 * lo, 2 * (hi - lo))]
                                      ).then_inc(index_ready, 1)

            def step(i, t, own, before):
                for tile, u in lagged(i, t, LAG_EMBED, own, before):
                    for half, (lo, hi) in enumerate(HALVES):
                        if u == hi - 1:
                            renew_index(tile, half)
                    norm_pair(tile, u)
                for tile, u in lagged(i, t, LAG_COPY_Z, own, before):
                    for s in z_after(u):
                        copy_z(tile, s)
                        if s % 2:
                            regroup_z(tile, s // 2)
                for tile, u in lagged(i, t, LAG_NORM_BANK, own, before):
                    for k in bank_after(u):
                        norm_bank(tile, k)
                for tile, u in lagged(i, t, LAG_SUM_BANK, own, before):
                    for k in bank_after(u):
                        sum_bank(tile, k)
                for tile, u in lagged(i, t, LAG_NORM_OUT, own, before):
                    if u == PAIRS - 1:
                        norm_out(tile)

            for t in range(PAIRS):
                if t == LAG_NORM_BANK + 1:
                    dve.wait_ge(x_ready, TILES)
                step(0, t, True, False)
                if t == DENSE_AT[0]:
                    dense_stats()
                if t == DENSE_AT[1] - 1:
                    dense_norm()
                if t == DENSE_AT[2]:
                    sum_dense()
                if t >= FOLD_AT + 5:
                    for qb in range(5 * (t - FOLD_AT - 5), min(QB, 5 * (t - FOLD_AT - 4))):
                        scale_wl(qb)
            finish_wl()
            with dve.Fori(1, TILES) as i:
                for t in range(PAIRS):
                    step(i, t, True, True)
            for t in range(PAIRS):
                step(TILES, t, False, True)

        @block.tensor
        def _(pe):
            pe.wait_ge(weights_ready, 1)
            nc.tensor.matmul(ps_m[0:PARTS * PARTS, 0:PR], ones_sb[:], wsit_c[:],
                             start=True, stop=True).then_inc(sc_summed, 1)

            def project_dense():
                pe.wait_ge(x_loaded, 16)
                pe.wait_ge(m_free, 1)
                for t in range(TILES):
                    for c in range(DK):
                        mm = nc.tensor.matmul(ps_m[:, t * E:(t + 1) * E], dense_sb[:, c, t * P:(t + 1) * P],
                                              wd_sb[:, c, :], start=(c == 0), stop=(c == DK - 1))
                mm.then_inc(x_projected, 1)

            def turn_dense():
                pe.wait_ge(x_hat_ready, TILES)
                for t in range(TILES):
                    mm = nc.tensor.transpose(ps_z[:, t * P:(t + 1) * P], x_hat[:, t, :], eye_sb[:])
                mm.then_inc(x_turned, 1)

            def sum_dense():
                pe.wait_ge(x_ready, TILES)
                nc.tensor.matmul(ps_z[DS_ROWS], ones_e[:], x_t[:].rearrange("p t g j -> p t j g"),
                                 start=True, stop=True).then_inc(dense_summed, 1)

            def turn_pair(i, t):
                n = PAIRS * i + t
                for c in (2 * t, 2 * t + 1):
                    pe.wait_ge(gathered[c], 16 * (i + 1))
                if behind(i, t, 2):
                    pe.wait_ge(pair_copied, n if t == 0 else n - 1)
                nc.tensor.transpose(ps_t[t % 2][:], emb[:, 2 * t:2 * t + 2, :].rearrange("p a b -> p (a b)"),
                                    eye_sb[:]).then_inc(pair_turned, 1)

            def embed_pair(i, t):
                n = PAIRS * i + t
                pe.wait_ge(pair_copied, n + 1)
                if behind(i, t, 2):
                    pe.wait_ge(y_normed, 2 * (n if t == 0 else n - 1))
                nc.tensor.matmul(ps_y[t % 2][:], emb_t[:, t, :], ws_c[:], start=True, stop=True
                                 ).then_inc(pair_embedded, 1)

            def project_bank(i, k):
                m = BANKS * i + k
                pieces = bank_pieces(k)
                pe.wait_ge(y_normed, CH * i + pieces[-1][0] + 1)
                if behind(i, k, 2):
                    pe.wait_ge(p_hat_ready, m - 1)
                out = ps_p[k % 2][:].rearrange("p (s q) -> p s q", q=PR)
                nc.tensor.matmul(out, bs_parts[:], sc_parts[:].rearrange("p (s q) -> p s q", s=1).broadcast_to(
                    [PARTS * PARTS, SPB, PR]), start=True, stop=True, skip_group_check=True)
                for c, b0, o0, nb in pieces:
                    mm = nc.tensor.matmul(out[:, o0:o0 + nb, :], y_norm[:, c, :],
                                          wsi_c[:, SPC * (c % PERIOD) + b0:SPC * (c % PERIOD) + b0 + nb, :],
                                          start=False, stop=True, skip_group_check=True)
                mm.then_inc(bank_projected, 1)

            def z_step(i, s):
                pe.wait_ge(p_hat_ready, BANKS * i + 2 * s + 2)
                if behind(i, s, 1):
                    pe.wait_ge(z_copied, ZSTEPS * i + s)
                for g in range(GZ):
                    for j in range(J):
                        b = J * (s * GZ + g) + j
                        mm = nc.tensor.matmul(ps_z[PR * j:PR * j + PR, g * NZ:(g + 1) * NZ],
                                              items[:, b, 2:IW], items[:, b, 0:NZ], start=True, stop=True)
                mm.then_inc(z_ready, 1)

            def fold_sums(qb):
                if qb == 0:
                    pe.wait_ge(wl_loaded, 32)
                mm = nc.tensor.matmul(ps_m[:], bsi_fold_sb[:, qb, :], wl_sb[:, qb, :],
                                      start=(qb == 0), stop=(qb == QB - 1))
                if qb == QB - 1:
                    mm.then_inc(sums_folded, 1)

            def fold_const():
                pe.wait_ge(sums_taken, 1)
                nc.tensor.matmul(ps_m[:], bsi_col_sb[:], sum_raw[:], start=True, stop=True
                                 ).then_inc(const_folded, 1)

            def interact(i, part):
                if part == 0:
                    pe.wait_ge(z_regrouped, 2 * (i + 1))
                    pe.wait_ge(m_free, i + 1)
                n = -(-QB // len(LAG_INTERACT))
                for q in range(n * part, min(n * part + n, QB)):
                    mm = nc.tensor.matmul(ps_m[:], z_qp[:, :, :, q].rearrange("p j g -> p (j g)"),
                                          wl_sb[:, q, :], start=(q == 0), stop=(q == QB - 1))
                if q == QB - 1:
                    mm.then_inc(o_ready, 1)

            def turn_out(i):
                pe.wait_ge(o_hat_ready, i + 1)
                for c in range(ZK):
                    mm = nc.tensor.transpose(ps_m[:, c * P:(c + 1) * P], o_hat[:, c * P:(c + 1) * P], eye_sb[:])
                mm.then_inc(o_turned, 1)

            def layer_1(i, part):
                if part == 0:
                    pe.wait_ge(z_t_ready, ZK * (i + 1))
                n = HK // len(LAG_LAYER_1)
                for m in range(n * part, n * part + n):
                    for c in range(ZK + DK):
                        rhs = z_t[:, c, :] if c < ZK else dense_sb[:, c - ZK, bass.ds(i * P, P)]
                        mm = nc.tensor.matmul(ps_m[:, m * P:(m + 1) * P], w1_sb[:, c, m * P:(m + 1) * P], rhs,
                                              start=(c == 0), stop=(c == ZK + DK - 1))
                if m == HK - 1:
                    mm.then_inc(h1_summed, 1)

            def layer_2(i):
                pe.wait_ge(h1_ready, HK * (i + 1))
                for m in range(H2 // P):
                    for c in range(HK):
                        mm = nc.tensor.matmul(ps_m[:, m * P:(m + 1) * P], w2_sb[:, c, m * P:(m + 1) * P],
                                              h1_t[:, c, :], start=(c == 0), stop=(c == HK - 1))
                mm.then_inc(h2_summed, 1)

            def layer_3(i):
                pe.wait_ge(h2_ready, H2 // P * (i + 1))
                for c in range(H2 // P):
                    mm = nc.tensor.matmul(ps_m[0:1, 0:P], w3_sb[:, c:c + 1], h2_t[:, c, :],
                                          start=(c == 0), stop=(c == H2 // P - 1))
                mm.then_inc(y_summed, 1)

            def step(i, t, own, before):
                for tile, u in lagged(i, t, LAG_TURN, own, before):
                    turn_pair(tile, u)
                for tile, u in lagged(i, t, LAG_EMBED, own, before):
                    embed_pair(tile, u)
                for tile, u in lagged(i, t, LAG_LAYER_2, own, before):
                    if u == PAIRS - 1:
                        layer_2(tile)
                for tile, u in lagged(i, t, LAG_Z, own, before):
                    for s in z_after(u):
                        z_step(tile, s)
                for tile, u in lagged(i, t, LAG_PROJECT, own, before):
                    for k in bank_after(u):
                        project_bank(tile, k)
                for part, lag in enumerate(LAG_INTERACT):
                    for tile, u in lagged(i, t, lag, own, before):
                        if u == PAIRS - 1:
                            interact(tile, part)
                for tile, u in lagged(i, t, LAG_TURN_OUT, own, before):
                    if u == PAIRS - 1:
                        turn_out(tile)
                for part, lag in enumerate(LAG_LAYER_1):
                    for tile, u in lagged(i, t, lag, own, before):
                        if u == PAIRS - 1:
                            layer_1(tile, part)
                for tile, u in lagged(i, t, LAG_LAYER_2, own, before):
                    if u == PAIRS - 1:
                        layer_3(tile)

            for t in range(PAIRS):
                if t == LAG_PROJECT + 1:
                    pe.wait_ge(weights_ready, 2)
                if t == LAG_Z + 3:
                    pe.wait_ge(x_summed, 1)
                step(0, t, True, False)
                if t == DENSE_AT[0] - 1:
                    project_dense()
                if t == DENSE_AT[1]:
                    turn_dense()
                if t == DENSE_AT[2]:
                    sum_dense()
                if t >= FOLD_AT:
                    for qb in range(2 * (t - FOLD_AT), min(QB, 2 * (t - FOLD_AT + 1))):
                        fold_sums(qb)
            fold_const()
            pe.wait_ge(wl_ready, 1)
            pe.wait_ge(top_loaded, 32)
            with pe.Fori(1, TILES) as i:
                for t in range(PAIRS):
                    step(i, t, True, True)
            for t in range(PAIRS):
                step(TILES, t, False, True)


def kernel(**inputs):
    import concourse.bacc as bacc
    from concourse.bass_utils import run_bass_kernel_spmd

    a = {k: np.asarray(v) for k, v in inputs.items()}
    arrays = {}

    base = np.concatenate([[0], np.cumsum(VOCAB)[:-1]]).astype(np.int32)
    rows = np.stack([a["ids"].reshape(-1), np.tile(base, B)])
    arrays["rows_at"] = np.ascontiguousarray(rows.reshape(2, TILES * CH, P).transpose(2, 0, 1))
    arrays["tables"] = np.concatenate([a[f"tbl_{t}"] for t in range(NT)], axis=0)

    consts = {}
    dense = a["r_dense_t"].T.reshape(DK, P, TILES, G, J).transpose(1, 0, 2, 4, 3)

    def k_major(w, k):
        return np.ascontiguousarray(w.reshape(k, P, -1).transpose(1, 0, 2))

    dense = np.concatenate([dense.reshape(P, DK, B), k_major(a["L0_rec_Wd"].T, DK)], axis=2)
    consts["gd"], consts["bd"] = a["L0_rec_gd"], a["L0_rec_bd"]
    consts["ws"] = np.zeros((2, D, 2, E), np.float32)
    for r in range(2):
        consts["ws"][r, :, r] = a["L0_rec_Ws"].T
    consts["gs"] = np.tile(a["L0_rec_gs"], (P, 1))
    consts["bs"] = np.tile(a["L0_rec_bs"], (PARTS * PARTS, 1))

    wsi_t = np.ascontiguousarray(a["L0_rec_Wsi"].T)
    blocks = np.zeros((P, PERIOD, SPC, PR), np.float32)
    for c in range(PERIOD):
        for r in range(P):
            sample, table = divmod(P * c + r, NT)
            blocks[r, c, sample - chunk_samples(c)[0]] = wsi_t[table]
    arrays["wsi_blocks"] = blocks.reshape(P, -1)
    arrays["dense"] = dense
    consts["wsi_t"] = wsi_t

    gsi, bsi, wl_t = a["L0_rec_gsi"], a["L0_rec_bsi"], a["L0_rec_Wl"].T
    slots = np.zeros((QA * QB, PR, MD), np.float32)
    gsi_q = np.ones((QA * QB, PR), np.float32)
    fold = np.zeros((QA * QB, PR, P), np.float32)
    dense_row = PR * DENSE_SUM_SLOT[0]
    for n, (hi, lo) in enumerate(zip(*np.tril_indices(NI, k=-1))):
        p, slot = hi - 1, lo + 1 if lo else 0
        slots[slot, p] = wl_t[n]
        if lo:
            fold[slot, p, p] = bsi[lo - 1]
            fold[slot, p, lo - 1] = bsi[p]
        else:
            fold[slot, p, dense_row] = bsi[p]
    for q in range(PR - 1):
        gsi_q[q + 2] = gsi[q]
    consts["gsi_p"] = np.ascontiguousarray(np.tile(gsi, QA).reshape(P, 1))
    consts["gsi_q"] = np.ascontiguousarray(gsi_q.reshape(QA, QB, PR).transpose(0, 2, 1)).reshape(P, QB)
    consts["bsi_col"] = np.zeros((PR, P), np.float32)
    consts["bsi_col"][:, dense_row] = bsi
    bsi_fold = np.ascontiguousarray(fold.reshape(QA, QB, PR, P).transpose(0, 2, 1, 3)
                                              ).reshape(P, QB, P)
    slots = slots.reshape(QA, QB, PR, MD).transpose(0, 2, 1, 3)
    arrays["wl_slots"] = np.ascontiguousarray(slots).reshape(P, QB, MD)
    arrays["bsi_fold"] = bsi_fold
    consts["gl"] = np.ascontiguousarray(a["L0_rec_gl"][:USED].reshape(ZK, P).T)
    consts["bl"] = np.ascontiguousarray(a["L0_rec_bl"][:USED].reshape(ZK, P).T)

    w1 = a["W_top1"]
    arrays["w1"] = k_major(np.concatenate([w1[:USED], w1[MD:]], axis=0), ZK + DK)
    consts["b1"] = np.ascontiguousarray(a["b_top1"].reshape(HK, P).T)
    arrays["w2"] = k_major(a["W_top2"], HK)
    consts["b2"] = np.ascontiguousarray(a["b_top2"].reshape(H2 // P, P).T)
    consts["w3"] = np.ascontiguousarray(a["W_top3"].reshape(H2 // P, P).T)

    consts["eye"] = np.eye(P, dtype=np.float32)
    masks = np.zeros((PARTS * PARTS, 2 * PARTS), np.float32)
    for r in range(PARTS * PARTS):
        masks[r, r // PARTS] = 1
        masks[r, PARTS + r % PARTS] = 1
    consts["part_masks"] = masks

    packed = {}
    for name, width in CONSTS.items():
        part = np.asarray(consts[name]).reshape(-1, width)
        packed[name] = np.zeros((P, width), np.float32)
        packed[name][:len(part)] = part
    arrays["consts"] = np.concatenate(list(packed.values()), axis=1)
    order = ("rows_at", "tables", "consts", "wsi_blocks", "dense", "wl_slots", "bsi_fold", "w1", "w2")
    arrays = {name: arrays[name] for name in order}

    nc = bacc.Bacc("TRN2", target_bir_lowering=False, num_devices=1)
    args = [nc.dram_tensor(f"in_{k}", v.shape, mybir.dt.from_np(v.dtype), kind="ExternalInput").ap()
            for k, v in arrays.items()]
    y_out = nc.dram_tensor("y_out", (1, B), F32, kind="ExternalOutput").ap()
    build(nc, *args, y_out)
    r = run_bass_kernel_spmd(nc, [{f"in_{k}": v for k, v in arrays.items()}], core_ids=[0])
    return r.results[0]["y_out"].reshape(B, 1)
```

```python
from contextlib import ExitStack

import numpy as np

import concourse.bass as bass
from concourse import mybir

ALU = mybir.AluOpType
ACT = mybir.ActivationFunctionType
AX = mybir.AxisListType
F32 = mybir.dt.float32
BF16 = mybir.dt.bfloat16
I32 = mybir.dt.int32

P = 128
EPS = 1e-5
B = 512
NT = 26
D = 64
E = 128
PR = 32
NI = PR + 1
DD = 256
MD = 512
USED = 384
H1, H2 = 512, 256
TILES = B // P
CH = NT * P // P
PAIRS = CH // 2
PERIOD = CH // 2
SPC = 6
SPB = 512 // PR
BANKS = P // SPB
J, G = 4, P // 4
IW = PR + 2
NZ = IW - 1
QA, QB = 4, 9
SUM_SLOT = divmod(1, QB)
DENSE_SUM_SLOT = divmod(NZ, QB)
CONST_SLOT = divmod(NZ + 1, QB)
GZ = 8
ZSTEPS = G // GZ
PARTS = 3
LAG_TURN, LAG_EMBED, LAG_PROJECT, LAG_SUM_BANK, LAG_NORM_BANK, LAG_Z, LAG_COPY_Z = 0, 1, 3, 4, 5, 6, 7
LAG_REGROUP_0 = (8, 9)
LAG_INTERACT, LAG_NORM_OUT, LAG_TURN_OUT = (8, 9), 9, 10
LAG_LAYER_1, LAG_LAYER_2 = (11, 12), 13
DENSE_AT = (2, 4, 5)
FOLD_AT = 5
FOLD_STEPS = -(-9 // 2)
DK, HK, ZK = DD // P, H1 // P, USED // P
CONSTS = {"ws": 2 * E, "gs": E, "wsi_t": PR, "wsi_rows": PERIOD * PR, "row_sample": PERIOD * SPC, "part_masks": 2 * PARTS, "bs": E, "eye": P, "gd": 1, "bd": 1,
          "gsi_p": 1, "gsi_q": QB, "bsi_col": P, "gl": ZK, "bl": ZK, "b1": HK, "b2": H2 // P, "w3": H2 // P}
VOCAB = [1250, 1000, 12500, 1000, 1250, 125000, 1000, 1000, 1250, 1250, 125000, 1250, 1250,
         125000, 12500, 12500, 1000, 12500, 1000, 1000, 12500, 1000, 12500, 12500, 1250, 1250]


def chunk_samples(c):
    return P * c // NT, (P * c + P - 1) // NT


def bank_pieces(k):
    half, kb = divmod(k, BANKS // 2)
    pieces = []
    for c in range(PERIOD):
        s0, s1 = chunk_samples(c)
        a, b = max(s0, SPB * kb), min(s1, SPB * kb + SPB - 1)
        if a <= b:
            pieces.append((half * PERIOD + c, a - s0, a - SPB * kb, b - a + 1))
    return pieces


def bank_after(u):
    return [k for k in range(BANKS) if bank_pieces(k)[-1][0] // 2 == u]


def z_after(u):
    return [k // 2 for k in bank_after(u) if k % 2]


def lagged(i, t, lag, own, before):
    if t >= lag:
        return [(i, t - lag)] if own else []
    return [(i - 1, t - lag + PAIRS)] if before else []


def behind(tile, n, depth):
    return not (isinstance(tile, int) and n < depth)


def build(nc, rows_at, tables, consts, dense, wl_slots, bsi_fold, w1, w2, y_out):
    with ExitStack() as ctx:
        def sb(name, shape, dt=F32):
            return ctx.enter_context(nc.sbuf_tensor(name, shape, dt))

        def psum(name, shape):
            return ctx.enter_context(nc.psum_tensor(name, shape, F32))

        def sem(name):
            return ctx.enter_context(nc.semaphore(name))

        consts_sb = sb("consts_sb", [P, sum(CONSTS.values())])

        def const(name, rows=P):
            names = list(CONSTS)
            at = sum(CONSTS[k] for k in names[:names.index(name)])
            return consts_sb[0:rows, at:at + CONSTS[name]]

        eye_sb = const("eye")
        ws_raw = const("ws").rearrange("p (r e) -> p r e", r=2)
        gs_sb, bs_sb = const("gs"), const("bs", PARTS * PARTS)
        wsi_raw = const("wsi_rows").rearrange("p (c q) -> p c q", q=PR)
        row_sample = const("row_sample")
        wsit_raw, masks_sb = const("wsi_t", NT), const("part_masks", PARTS * PARTS)
        gd_sb, bd_sb, gl_sb, bl_sb = const("gd"), const("bd"), const("gl"), const("bl")
        gsi_p_sb, gsi_q_sb = const("gsi_p"), const("gsi_q")
        bsi_col_sb = const("bsi_col", PR)
        b1_sb, b2_sb, w3_sb = const("b1"), const("b2"), const("w3")
        rows_sb = sb("rows_sb", [P, 2, TILES * CH], I32)
        row_index = sb("row_index", [P, (TILES + 1) * CH], I32)
        tile_index = sb("tile_index", [P, CH], I32)
        ws_mean = sb("ws_mean", [P, 2])
        ws_c = sb("ws_c", [P, 2, E])
        wsi_mean = sb("wsi_mean", [P, PERIOD])
        wsi_rows = sb("wsi_rows", [P, PERIOD, PR])
        wsi_c = sb("wsi_c", [P, PERIOD * SPC, PR])
        wsit_mean = sb("wsit_mean", [NT, 1])
        wsit_c = sb("wsit_c", [NT, PR])
        ones_sb = sb("ones_sb", [NT, PARTS * PARTS])
        sc_sb = sb("sc_sb", [PARTS * PARTS, PR])
        bs_parts = sb("bs_parts", [PARTS * PARTS, E], BF16)
        sc_parts = sb("sc_parts", [PARTS * PARTS, PR], BF16)
        split_hi = sb("split_hi", [PARTS * PARTS, 2, PARTS, E], BF16)
        split_f = sb("split_f", [PARTS * PARTS, 2, 4, E])
        gsi_pq = sb("gsi_pq", [P, QB])
        bsi_fold_sb = sb("bsi_fold_sb", [P, QB, P])
        sum_raw = sb("sum_raw", [PR, MD])
        ones_e = sb("ones_e", [P, PR])
        dense_sum = sb("dense_sum", [P, TILES, G])
        wl_sb = sb("wl_sb", [P, QB, MD])
        w1_sb = sb("w1_sb", [P, ZK + DK, H1])
        w2_sb = sb("w2_sb", [P, HK, H2])
        eps_sb = sb("eps_sb", [P, 1])
        warm_sb = sb("warm_sb", [P, 1])
        dense_wd = sb("dense_wd", [P, DK, B + E])
        dense_sb, wd_sb = dense_wd[:, :, 0:B], dense_wd[:, :, B:B + E]
        x_stats = sb("x_stats", [P, TILES, 6])
        x_mv = sb("x_mv", [P, TILES, 2])
        x_std = sb("x_std", [P, TILES])
        x_rstd = sb("x_rstd", [P, TILES])
        x_hat = sb("x_hat", [P, TILES, E])
        x_t = sb("x_t", [P, TILES, G, J])
        emb = sb("emb", [P, CH, D])
        emb_t = sb("emb_t", [P, PAIRS, P])
        sq_junk = sb("sq_junk", [P, 2, E])
        y_var = sb("y_var", [P, CH])
        y_std = sb("y_std", [P, CH])
        y_rstd = sb("y_rstd", [P, CH])
        y_norm = sb("y_norm", [P, CH, E])
        proj_sq = sb("proj_sq", [P, 2, SPB * PR])
        p_var = sb("p_var", [P, BANKS, SPB])
        p_std = sb("p_std", [P, BANKS, SPB])
        p_rstd = sb("p_rstd", [P, BANKS, SPB])
        items = sb("items", [P, P, IW])
        z_jp = sb("z_jp", [P, QA, G, QB])
        z_qp = sb("z_qp", [P, J, G, QB])
        o_stats = sb("o_stats", [P, 6])
        o_mv = sb("o_mv", [P, 2])
        o_std = sb("o_std", [P, 1])
        o_rstd = sb("o_rstd", [P, 1])
        o_hat = sb("o_hat", [P, USED])
        z_t = sb("z_t", [P, ZK, P])
        h1_t = sb("h1_t", [P, HK, P])
        h2_t = sb("h2_t", [P, H2 // P, P])
        y_sb = sb("y_sb", [1, TILES, G, J])

        ps_t = [psum(f"ps_t{r}", [P, P]) for r in range(2)]
        ps_y = [psum(f"ps_y{r}", [P, 2, E]) for r in range(2)]
        ps_p = [psum(f"ps_p{r}", [P, SPB * PR]) for r in range(2)]
        ps_z = psum("ps_z", [P, 512])
        ps_m = psum("ps_m", [P, 512])

        def y_bank(u):
            return ps_m[:, 0:2 * E].rearrange("p (r e) -> p r e", r=2) if u == PAIRS - 1 else ps_y[u % 2][:]

        rows_loaded = sem("rows_loaded")
        consts_loaded = sem("consts_loaded")
        x_loaded = sem("x_loaded")
        wl_loaded = sem("wl_loaded")
        top_loaded = sem("top_loaded")
        index_ready = sem("index_ready")
        dve_prep = sem("dve_prep")
        wsi_placed = sem("wsi_placed")
        eps_ready = sem("eps_ready")
        weights_ready = sem("weights_ready")
        sc_summed = sem("sc_summed")
        x_projected = sem("x_projected")
        x_std_ready = sem("x_std_ready")
        x_stats_ready = sem("x_stats_ready")
        x_hat_ready = sem("x_hat_ready")
        x_counted = sem("x_counted")
        x_rstd_ready = sem("x_rstd_ready")
        x_turned = sem("x_turned")
        x_ready = sem("x_ready")
        gathered = [sem(f"gathered{c}") for c in range(CH)]
        pair_turned = sem("pair_turned")
        pair_copied = sem("pair_copied")
        pair_embedded = sem("pair_embedded")
        y_squared = sem("y_squared")
        y_std_ready = sem("y_std_ready")
        y_rstd_ready = sem("y_rstd_ready")
        y_normed = sem("y_normed")
        bank_projected = sem("bank_projected")
        bank_squared = sem("bank_squared")
        p_var_ready = sem("p_var_ready")
        p_std_ready = sem("p_std_ready")
        p_rstd_ready = sem("p_rstd_ready")
        p_hat_ready = sem("p_hat_ready")
        dense_summed = sem("dense_summed")
        sums_folded = sem("sums_folded")
        const_folded = sem("const_folded")
        z_ready = sem("z_ready")
        z_copied = sem("z_copied")
        z_moved = sem("z_moved")
        sums_taken = sem("sums_taken")
        x_summed = sem("x_summed")
        z_regrouped_act = sem("z_regrouped_act")
        z_regrouped_dve = sem("z_regrouped_dve")
        m_free = sem("m_free")
        o_ready = sem("o_ready")
        o_stats_ready = sem("o_stats_ready")
        o_mv_ready = sem("o_mv_ready")
        o_std_ready = sem("o_std_ready")
        o_rstd_ready = sem("o_rstd_ready")
        o_hat_ready = sem("o_hat_ready")
        o_turned = sem("o_turned")
        z_t_ready = sem("z_t_ready")
        h1_summed = sem("h1_summed")
        h1_ready = sem("h1_ready")
        h2_summed = sem("h2_summed")
        h2_ready = sem("h2_ready")
        y_summed = sem("y_summed")
        y_stored = sem("y_stored")

        DS_ROWS = slice(PR * DENSE_SUM_SLOT[0], PR * DENSE_SUM_SLOT[0] + PR)
        REGROUP = ((slice(0, G - GZ), ZSTEPS - 1), (slice(G - GZ, G), ZSTEPS))
        ACT_JS, DVE_JS = (0, 1), (2, 3)
        REGROUPED_ACT = QA * (J + len(ACT_JS))
        REGROUPED_DVE = QA * len(DVE_JS)
        WL_PIECE = 3
        HALVES = ((0, 7), (7, PAIRS))

        block = ctx.enter_context(nc.Block())

        @block.sync
        def _(sp):
            sp.dma_start(rows_sb[:], rows_at).then_inc(rows_loaded, 16)
            sp.dma_start(consts_sb[:], consts).then_inc(consts_loaded, 16)
            sp.dma_start(dense_wd[:], dense).then_inc(x_loaded, 16)
            for q in range(0, QB, WL_PIECE):
                sp.wait_ge(pair_turned, 1 + q // WL_PIECE)
                sp.dma_start(wl_sb[:, q:q + WL_PIECE, :], wl_slots[:, q:q + WL_PIECE, :]).then_inc(wl_loaded, 16)
            sp.wait_ge(pair_turned, 1 + QB // WL_PIECE)
            sp.dma_start(bsi_fold_sb[:], bsi_fold).then_inc(wl_loaded, 16)
            for n in range(2):
                half = slice(n * (ZK + DK) // 2, (n + 1) * (ZK + DK) // 2)
                sp.wait_ge(pair_turned, 2 + n + QB // WL_PIECE)
                sp.dma_start(w1_sb[:, half, :], w1[:, half, :]).then_inc(top_loaded, 16)
            sp.dma_start(w2_sb[:], w2).then_inc(top_loaded, 16)
            sp.wait_ge(m_free, TILES + 2)
            sp.dma_start(y_out, y_sb[:].rearrange("p a b c -> p (a b c)")).then_inc(y_stored, 16)
            sp.wait_ge(y_stored, 16)

        @block.gpsimd
        def _(pool):
            halves = pool.alloc_register("halves")
            pool.reg_mov(halves, 1)

            def gather():
                for c in range(CH):
                    for half, (lo, hi) in enumerate(HALVES):
                        if c == 2 * lo:
                            pool.wait_ge(index_ready, halves)
                            pool.reg_add(halves, halves, 1)
                    pool.indirect_dma_start(
                        out=emb[:, c, :], out_offset=None, in_=tables,
                        in_offset=bass.IndirectOffsetOnAxis(
                            ap=tile_index[:, c:c + 1], axis=0),
                    ).then_inc(gathered[c], 16)

            with pool.Fori(0, TILES):
                gather()

        @block.scalar
        def _(act):
            def std_dense():
                act.wait_ge(x_stats_ready, TILES)
                nc.scalar.activation(x_std[:].rearrange("p (t a) -> p t a", a=1), x_mv[:, :, 1:2], ACT.Sqrt,
                                     bias=eps_sb[:, 0:1]).then_inc(x_std_ready, 1)

            def scale_dense():
                act.wait_ge(x_turned, 1)
                for t in range(TILES):
                    nc.scalar.activation(x_t[:, t].rearrange("p g j -> p j g"),
                                         ps_z[:, t * P:(t + 1) * P].rearrange("p (j g) -> p j g", j=J),
                                         ACT.Identity, bias=bd_sb[:, 0:1], scale=gd_sb[:, 0:1]
                                         ).then_inc(x_ready, 1)

            def copy_pair(i, t):
                n = PAIRS * i + t
                act.wait_ge(pair_turned, n + 1)
                if behind(i, t, 4):
                    act.wait_ge(pair_embedded, n - 3)
                nc.scalar.copy(emb_t[:, t, :], ps_t[t % 2][:]).then_inc(pair_copied, 1)

            def square_pair(i, t):
                n = PAIRS * i + t
                act.wait_ge(pair_embedded, n + 1)
                for r in range(2):
                    nc.scalar.activation(sq_junk[:, r, :], y_bank(t)[:, r, :], ACT.Square,
                                         scale=float(E) ** -0.5,
                                         accum_out=y_var[:, 2 * t + r:2 * t + r + 1]
                                         ).then_inc(y_squared, 1)
                act.wait_ge(y_squared, 2 * n + 2)
                if behind(i, t, 4):
                    act.wait_ge(y_rstd_ready, n - 3)
                nc.scalar.activation(y_std[:, 2 * t:2 * t + 2], y_var[:, 2 * t:2 * t + 2], ACT.Sqrt,
                                     bias=eps_sb[:, 0:1]).then_inc(y_std_ready, 1)

            def square_bank(i, k):
                m = BANKS * i + k
                act.wait_ge(bank_projected, m + 1)
                if behind(i, k, 2):
                    act.wait_ge(p_var_ready, m - 1)
                nc.scalar.activation(proj_sq[:, k % 2, :], ps_p[k % 2][:], ACT.Square,
                                     scale=float(PR) ** -0.5).then_inc(bank_squared, 1)

            def std_bank(i, k):
                m = BANKS * i + k
                act.wait_ge(p_var_ready, m + 1)
                if behind(i, k, 4):
                    act.wait_ge(p_rstd_ready, m - 3)
                nc.scalar.activation(p_std[:, k, :], p_var[:, k, :], ACT.Sqrt,
                                     bias=eps_sb[:, 0:1]).then_inc(p_std_ready, 1)

            def regroup_z(i, part, js):
                groups, steps = REGROUP[part]
                act.wait_ge(z_copied, ZSTEPS * i + steps)
                if part == 0 and behind(i, 0, 1):
                    act.wait_ge(o_ready, i)
                for j in js:
                    for qa in range(QA):
                        nc.scalar.copy(z_qp[PR * qa:PR * qa + PR, j, groups, :],
                                       z_jp[PR * j:PR * j + PR, qa, groups, :]
                                       ).then_inc(z_regrouped_act, 1)

            def std_out(i):
                act.wait_ge(o_mv_ready, i + 1)
                nc.scalar.activation(o_std[:], o_mv[:, 1:2], ACT.Sqrt,
                                     bias=eps_sb[:, 0:1]).then_inc(o_std_ready, 1)

            def scale_z(i):
                act.wait_ge(o_turned, i + 1)
                for c in range(ZK):
                    nc.scalar.activation(z_t[:, c, :], ps_m[:, c * P:(c + 1) * P], ACT.Identity,
                                         bias=bl_sb[:, c:c + 1], scale=gl_sb[:, c:c + 1]
                                         ).then_inc(z_t_ready, 1)

            def relu_1(i, part):
                n = HK // len(LAG_LAYER_1)
                act.wait_ge(h1_summed, len(LAG_LAYER_1) * i + part + 1)
                for c in range(n * part, n * part + n):
                    nc.scalar.activation(h1_t[:, c, :], ps_m[:, c * P:(c + 1) * P], ACT.Relu,
                                         bias=b1_sb[:, c:c + 1]).then_inc(h1_ready, 1)

            def relu_2(i):
                act.wait_ge(h2_summed, i + 1)
                for c in range(H2 // P):
                    nc.scalar.activation(h2_t[:, c, :], ps_m[:, c * P:(c + 1) * P], ACT.Relu,
                                         bias=b2_sb[:, c:c + 1]).then_inc(h2_ready, 1)

            def copy_y(i):
                act.wait_ge(y_summed, i + 1)
                nc.scalar.copy(y_sb[0:1, bass.ds(i, 1)].rearrange("p a g j -> p a j g"),
                               ps_m[0:1, 0:P].rearrange("p (a j g) -> p a j g", a=1, j=J)
                               ).then_inc(m_free, 1)

            def step(i, t, own, before):
                for tile, u in lagged(i, t, LAG_NORM_BANK, own, before):
                    for k in bank_after(u):
                        std_bank(tile, k)
                for tile, u in lagged(i, t, LAG_TURN, own, before):
                    copy_pair(tile, u)
                for tile, u in lagged(i, t, LAG_SUM_BANK, own, before):
                    for k in bank_after(u):
                        square_bank(tile, k)
                for tile, u in lagged(i, t, LAG_EMBED, own, before):
                    square_pair(tile, u)
                for n, lag in enumerate(LAG_REGROUP_0):
                    for tile, u in lagged(i, t, lag, own, before):
                        if z_after(u) == [ZSTEPS - 2]:
                            regroup_z(tile, 0, (2 * n, 2 * n + 1))
                for tile, u in lagged(i, t, LAG_COPY_Z, own, before):
                    if z_after(u) == [ZSTEPS - 1]:
                        regroup_z(tile, 1, ACT_JS)
                for part, lag in enumerate(LAG_LAYER_1):
                    for tile, u in lagged(i, t, lag, own, before):
                        if u == PAIRS - 1:
                            relu_1(tile, part)
                for lag, work in ((LAG_NORM_OUT, std_out), (LAG_TURN_OUT, scale_z),
                                  (LAG_LAYER_2, relu_2), (LAG_LAYER_2, copy_y)):
                    for tile, u in lagged(i, t, lag, own, before):
                        if u == PAIRS - 1:
                            work(tile)

            act.wait_ge(eps_ready, 1)
            nc.scalar.activation(warm_sb[:], eps_sb[:], ACT.Sqrt)
            for t in range(PAIRS):
                step(0, t, True, False)
                if t == DENSE_AT[0]:
                    std_dense()
                if t == DENSE_AT[1]:
                    scale_dense()
            with act.Fori(1, TILES) as i:
                for t in range(PAIRS):
                    step(i, t, True, True)
            for t in range(PAIRS):
                step(TILES, t, False, True)

        @block.vector
        def _(dve):
            chain = [0]

            def link(ins):
                chain[0] += 1
                ins.then_inc(dve_prep, 1)
                dve.wait_ge(dve_prep, chain[0])

            nc.vector.memset(eps_sb[:], EPS).then_inc(eps_ready, 1)
            dve.wait_ge(rows_loaded, 16)
            nc.vector.memset(row_index[:, TILES * CH:], 0)
            link(nc.vector.tensor_tensor(row_index[:, 0:TILES * CH], rows_sb[:, 0, :], rows_sb[:, 1, :], ALU.add))
            nc.vector.tensor_copy(tile_index[:], row_index[:, 0:CH]).then_inc(index_ready, len(HALVES))
            nc.vector.memset(z_jp[:, QA - 1, :, NZ - (QA - 1) * QB:QB], 1.0)
            nc.vector.memset(items[:, :, 1], 1.0)
            nc.vector.memset(ones_e[:], 1.0)
            nc.vector.memset(ones_sb[:], 1.0)
            dve.wait_ge(consts_loaded, 16)
            link(nc.vector.tensor_reduce(ws_mean[:], ws_raw[:], AX.X, ALU.add))
            link(nc.vector.tensor_scalar(ws_mean[:], ws_mean[:], 1.0 / E, None, ALU.mult))
            link(nc.vector.tensor_tensor(ws_c[:], ws_raw[:],
                                         ws_mean[:].rearrange("p (a b) -> p a b", b=1).broadcast_to([P, 2, E]),
                                         ALU.subtract))
            link(nc.vector.tensor_reduce(wsit_mean[:], wsit_raw[:], AX.X, ALU.add))
            link(nc.vector.tensor_scalar(wsit_mean[:], wsit_mean[:], 1.0 / PR, None, ALU.mult))
            link(nc.vector.tensor_scalar(wsit_c[:], wsit_raw[:], wsit_mean[:, 0:1], None, ALU.subtract))
            nc.vector.tensor_copy(wsit_mean[:], wsit_mean[:]).then_inc(weights_ready, 1)
            link(nc.vector.tensor_reduce(wsi_mean[:], wsi_raw, AX.X, ALU.add))
            link(nc.vector.tensor_scalar(wsi_mean[:], wsi_mean[:], 1.0 / PR, None, ALU.mult))
            link(nc.vector.tensor_tensor(wsi_rows[:], wsi_raw,
                                         wsi_mean[:].rearrange("p (a b) -> p a b", b=1).broadcast_to(
                                             [P, PERIOD, PR]), ALU.subtract))

            dve.wait_ge(sc_summed, 1)
            nc.vector.tensor_copy(sc_sb[:], ps_m[0:PARTS * PARTS, 0:PR]).then_inc(m_free, 1)
            dve.wait_ge(m_free, 1)

            def place_wsi(k):
                lo = bank_pieces(k - 1)[-1][0] + 1 if k else 0
                hi = bank_pieces(k)[-1][0] + 1
                blocks = slice(SPC * lo, SPC * hi)
                nc.vector.tensor_tensor(
                    wsi_c[:, blocks, :].rearrange("p (c s) q -> p c s q", s=SPC),
                    wsi_rows[:, lo:hi, :].rearrange("p c (s q) -> p c s q", s=1).broadcast_to(
                        [P, hi - lo, SPC, PR]),
                    row_sample[:, blocks].rearrange("p (c s q) -> p c s q", s=SPC, q=1).broadcast_to(
                        [P, hi - lo, SPC, PR]), ALU.mult).then_inc(wsi_placed, 1)

            def split_bias():
                sides = ((bs_sb, bs_parts, E), (sc_sb, sc_parts, PR))
                rest, total = [bs_sb, sc_sb[:]], [None, None]
                for q in range(PARTS):
                    for side, (_, _, n) in enumerate(sides):
                        last = nc.vector.tensor_copy(split_hi[:, side, q, 0:n], rest[side])
                    link(last)
                    for side, (_, dst, n) in enumerate(sides):
                        hi = split_hi[:, side, q, 0:n]
                        if q < PARTS - 1:
                            left = split_f[:, side, q, 0:n]
                            nc.vector.tensor_tensor(left, rest[side], hi, ALU.subtract)
                            rest[side] = left
                        mask = masks_sb[:, PARTS * side + q:PARTS * side + q + 1]
                        into = dst[:, 0:n] if q == PARTS - 1 else split_f[:, side, 2 + q, 0:n]
                        if q == 0:
                            last = nc.vector.tensor_scalar(into, hi, mask, None, ALU.mult)
                        else:
                            last = nc.vector.scalar_tensor_tensor(out=into, in0=hi, scalar=mask, in1=total[side],
                                                                  op0=ALU.mult, op1=ALU.add)
                        total[side] = into
                    link(last)
                nc.vector.tensor_copy(wsit_mean[:], wsit_mean[:]).then_inc(weights_ready, 1)

            def dense_stats():
                dve.wait_ge(x_projected, 1)
                for t in range(TILES):
                    nc.vector.bn_stats(x_stats[:, t, :], ps_m[:, t * E:(t + 1) * E]).then_inc(x_counted, 1)
                for t in range(TILES):
                    dve.wait_ge(x_counted, t + 1)
                    nc.vector.bn_aggr(x_mv[:, t, :], x_stats[:, t, :]).then_inc(x_stats_ready, 1)

            def dense_norm():
                dve.wait_ge(x_std_ready, 1)
                nc.vector.reciprocal(x_rstd[:], x_std[:]).then_inc(x_rstd_ready, 1)
                dve.wait_ge(x_rstd_ready, 1)
                for t in range(TILES):
                    nc.vector.tensor_scalar(x_hat[:, t, :], ps_m[:, t * E:(t + 1) * E], x_mv[:, t, 0:1],
                                            x_rstd[:, t:t + 1], ALU.subtract, ALU.mult).then_inc(x_hat_ready, 1)

            def sum_dense():
                dve.wait_ge(dense_summed, 1)
                nc.vector.tensor_copy(dense_sum[:].rearrange("p t g -> p (t g)"), ps_z[:, 0:B // J]
                                      ).then_inc(x_summed, 1)
                dve.wait_ge(x_summed, 1)

            def take_sums():
                dve.wait_ge(wl_loaded, 16 * (QB // WL_PIECE + 1))
                link(nc.vector.tensor_scalar(gsi_pq[:], gsi_q_sb[:], gsi_p_sb[:, 0:1], None, ALU.mult))
                link(nc.vector.tensor_scalar(bsi_col_sb[:], bsi_col_sb[:], float(E) / 2, None, ALU.mult))
                dve.wait_ge(sums_folded, 1)
                link(nc.vector.tensor_copy(sum_raw[:], ps_m[0:PR, :]))
                scale_wl((SUM_SLOT[1], DENSE_SUM_SLOT[1], CONST_SLOT[1]))
                (qa, qb) = SUM_SLOT
                nc.vector.tensor_scalar(wl_sb[PR * qa:PR * qa + PR, qb, :], sum_raw[:], gsi_p_sb[0:PR, 0:1],
                                        None, ALU.mult)
                nc.vector.tensor_copy(wl_sb[DS_ROWS, DENSE_SUM_SLOT[1], :], ps_m[DS_ROWS]
                                      ).then_inc(sums_taken, 1)

            def scale_wl(slots):
                for qb in slots:
                    last = nc.vector.tensor_scalar(wl_sb[:, qb, :], wl_sb[:, qb, :], gsi_pq[:, qb:qb + 1], None,
                                                   ALU.mult)
                link(last)

            def take_const():
                dve.wait_ge(const_folded, 1)
                nc.vector.tensor_copy(wl_sb[DS_ROWS, CONST_SLOT[1], :], ps_m[DS_ROWS]).then_inc(m_free, 1)

            def norm_pair(i, t):
                n = PAIRS * i + t
                dve.wait_ge(y_std_ready, n + 1)
                nc.vector.reciprocal(y_rstd[:, 2 * t:2 * t + 2], y_std[:, 2 * t:2 * t + 2]
                                     ).then_inc(y_rstd_ready, 1)
                dve.wait_ge(y_rstd_ready, n + 1)
                if t >= 8:
                    dve.wait_ge(bank_projected, BANKS * i + 1)
                elif behind(i, t, PAIRS):
                    reader = max(k for k in range(BANKS) if bank_pieces(k)[0][0] <= 2 * t + 1)
                    dve.wait_ge(bank_projected, BANKS * (i - 1) + reader + 1)
                for r in range(2):
                    c = 2 * t + r
                    nc.vector.scalar_tensor_tensor(out=y_norm[:, c, :], in0=y_bank(t)[:, r, :],
                                                   scalar=y_rstd[:, c:c + 1], in1=gs_sb[:],
                                                   op0=ALU.mult, op1=ALU.mult).then_inc(y_normed, 1)

            def sum_bank(i, k):
                m = BANKS * i + k
                dve.wait_ge(bank_squared, m + 1)
                if behind(i, k, 4):
                    dve.wait_ge(p_std_ready, m - 3)
                nc.vector.tensor_reduce(p_var[:, k, :],
                                        proj_sq[:, k % 2, :].rearrange("p (s q) -> p s q", q=PR),
                                        AX.X, ALU.add).then_inc(p_var_ready, 1)

            def norm_bank(i, k):
                m = BANKS * i + k
                dve.wait_ge(p_std_ready, m + 1)
                nc.vector.reciprocal(p_rstd[:, k, :], p_std[:, k, :]).then_inc(p_rstd_ready, 1)
                s = k // 2
                if s >= ZSTEPS // 2:
                    dve.wait_ge(z_ready, ZSTEPS * i + 1)
                elif behind(i, s, ZSTEPS):
                    dve.wait_ge(z_ready, ZSTEPS * (i - 1) + s + 1)
                if k % 2 == 0:
                    nc.vector.tensor_copy(
                        items[:, k * SPB:(k + 2) * SPB, 0],
                        x_t[:, bass.ds(i, 1), s * GZ:(s + 1) * GZ].rearrange("p a g j -> p (a g j)"))
                dve.wait_ge(p_rstd_ready, m + 1)
                nc.vector.tensor_tensor(
                    items[:, k * SPB:(k + 1) * SPB, 2:IW], ps_p[k % 2][:].rearrange("p (s q) -> p s q", q=PR),
                    p_rstd[:, k, :].rearrange("p (s q) -> p s q", q=1).broadcast_to([P, SPB, PR]),
                    ALU.mult).then_inc(p_hat_ready, 1)

            def copy_z(i, s):
                dve.wait_ge(z_ready, ZSTEPS * i + s + 1)
                if s == 0 and behind(i, s, ZSTEPS):
                    dve.wait_ge(z_regrouped_act, REGROUPED_ACT * i)
                    dve.wait_ge(z_regrouped_dve, REGROUPED_DVE * i)
                z = ps_z[:, 0:GZ * NZ].rearrange("p (g q) -> p g q", q=NZ)
                full = (QA - 1) * QB
                nc.vector.tensor_copy(z_jp[:, DENSE_SUM_SLOT[0], s * GZ:(s + 1) * GZ, DENSE_SUM_SLOT[1]],
                                      dense_sum[:, bass.ds(i, 1), s * GZ:(s + 1) * GZ].rearrange("p a g -> p (a g)"))
                nc.vector.tensor_copy(z_jp[:, 0:QA - 1, s * GZ:(s + 1) * GZ, :],
                                      z[:, :, 0:full].rearrange("p g (a b) -> p a g b", b=QB))
                nc.vector.tensor_copy(z_jp[:, QA - 1, s * GZ:(s + 1) * GZ, 0:NZ - full],
                                      z[:, :, full:NZ]).then_inc(z_copied, 1)

            def regroup_z(i):
                groups, _ = REGROUP[1]
                dve.wait_ge(z_copied, ZSTEPS * (i + 1))
                for j in DVE_JS:
                    for qa in range(QA):
                        nc.vector.tensor_copy(z_qp[PR * qa:PR * qa + PR, j, groups, :],
                                              z_jp[PR * j:PR * j + PR, qa, groups, :]
                                              ).then_inc(z_regrouped_dve, 1)

            def norm_out(i):
                dve.wait_ge(o_ready, i + 1)
                nc.vector.bn_stats(o_stats[:], ps_m[:]).then_inc(o_stats_ready, 1)
                counted = i + 1 if isinstance(i, int) else dve.snap(i + 1)
                dve.wait_ge(o_stats_ready, 1)
                dve.wait_ge(o_stats_ready, counted)
                nc.vector.bn_aggr(o_mv[:], o_stats[:]).then_inc(o_mv_ready, 1)
                dve.wait_ge(o_std_ready, i + 1)
                nc.vector.reciprocal(o_rstd[:], o_std[:]).then_inc(o_rstd_ready, 1)
                dve.wait_ge(o_rstd_ready, i + 1)
                nc.vector.tensor_scalar(o_hat[:], ps_m[:, 0:USED], o_mv[:, 0:1], o_rstd[:, 0:1],
                                        ALU.subtract, ALU.mult).then_inc(o_hat_ready, 1)

            def renew_index(i, half):
                lo, hi = HALVES[half]
                dve.wait_ge(pair_turned, PAIRS * i + hi)
                nc.vector.tensor_copy(tile_index[:, 2 * lo:2 * hi],
                                      row_index[:, bass.ds((i + 1) * CH + 2 * lo, 2 * (hi - lo))]
                                      ).then_inc(index_ready, 1)

            def step(i, t, own, before):
                for tile, u in lagged(i, t, LAG_NORM_BANK, own, before):
                    for k in bank_after(u):
                        norm_bank(tile, k)
                for tile, u in lagged(i, t, LAG_COPY_Z, own, before):
                    for s in z_after(u):
                        copy_z(tile, s)
                        if s == ZSTEPS - 1:
                            regroup_z(tile)
                for tile, u in lagged(i, t, LAG_EMBED, own, before):
                    for half, (lo, hi) in enumerate(HALVES):
                        if u == hi - 1:
                            renew_index(tile, half)
                for tile, u in lagged(i, t, LAG_SUM_BANK, own, before):
                    for k in bank_after(u):
                        sum_bank(tile, k)
                for tile, u in lagged(i, t, LAG_EMBED, own, before):
                    norm_pair(tile, u)
                for tile, u in lagged(i, t, LAG_NORM_OUT, own, before):
                    if u == PAIRS - 1:
                        norm_out(tile)

            for t in range(PAIRS):
                if t == LAG_NORM_BANK + 1:
                    dve.wait_ge(x_ready, TILES)
                step(0, t, True, False)
                if t == LAG_EMBED:
                    split_bias()
                if t < BANKS // 2:
                    place_wsi(t)
                if t == DENSE_AT[0]:
                    dense_stats()
                if t == DENSE_AT[1] - 1:
                    dense_norm()
                if t == DENSE_AT[2]:
                    sum_dense()
                if t == FOLD_AT + FOLD_STEPS:
                    take_sums()
                if t == FOLD_AT + FOLD_STEPS + 1:
                    plain = [qb for qb in range(QB)
                             if qb not in (SUM_SLOT[1], DENSE_SUM_SLOT[1], CONST_SLOT[1])]
                    scale_wl(plain)
                    take_const()
            with dve.Fori(1, TILES) as i:
                for t in range(PAIRS):
                    step(i, t, True, True)
            for t in range(PAIRS):
                step(TILES, t, False, True)

        @block.tensor
        def _(pe):
            pe.wait_ge(weights_ready, 1)
            nc.tensor.matmul(ps_m[0:PARTS * PARTS, 0:PR], ones_sb[:], wsit_c[:],
                             start=True, stop=True).then_inc(sc_summed, 1)

            def project_dense():
                pe.wait_ge(x_loaded, 16)
                pe.wait_ge(m_free, 1)
                for t in range(TILES):
                    for c in range(DK):
                        mm = nc.tensor.matmul(ps_m[:, t * E:(t + 1) * E], dense_sb[:, c, t * P:(t + 1) * P],
                                              wd_sb[:, c, :], start=(c == 0), stop=(c == DK - 1))
                mm.then_inc(x_projected, 1)

            def turn_dense():
                pe.wait_ge(x_hat_ready, TILES)
                for t in range(TILES):
                    mm = nc.tensor.transpose(ps_z[:, t * P:(t + 1) * P], x_hat[:, t, :], eye_sb[:])
                mm.then_inc(x_turned, 1)

            def sum_dense():
                pe.wait_ge(x_ready, TILES)
                for j in range(J):
                    mm = nc.tensor.matmul(ps_z[PR * j:PR * j + PR, 0:B // J].rearrange("p (t g) -> p t g", g=G),
                                          ones_e[:], x_t[:, :, :, j], start=True, stop=True)
                mm.then_inc(dense_summed, 1)

            def turn_pair(i, t):
                n = PAIRS * i + t
                for c in (2 * t, 2 * t + 1):
                    pe.wait_ge(gathered[c], 16 * (i + 1))
                if behind(i, t, 2):
                    pe.wait_ge(pair_copied, n if t == 0 else n - 1)
                nc.tensor.transpose(ps_t[t % 2][:], emb[:, 2 * t:2 * t + 2, :].rearrange("p a b -> p (a b)"),
                                    eye_sb[:]).then_inc(pair_turned, 1)

            def embed_pair(i, t):
                n = PAIRS * i + t
                pe.wait_ge(pair_copied, n + 1)
                if t == PAIRS - 1:
                    pe.wait_ge(m_free, i + 2)
                elif behind(i, t, 2):
                    pe.wait_ge(y_normed, 2 * (n - 2 if t < 2 else n - 1))
                nc.tensor.matmul(y_bank(t), emb_t[:, t, :], ws_c[:], start=True, stop=True
                                 ).then_inc(pair_embedded, 1)

            def project_bank(i, k):
                m = BANKS * i + k
                pieces = bank_pieces(k)
                pe.wait_ge(y_normed, CH * i + pieces[-1][0] + 1)
                if isinstance(i, int) and i == 0 and k < BANKS // 2:
                    pe.wait_ge(wsi_placed, k + 1)
                if behind(i, k, 2):
                    pe.wait_ge(p_hat_ready, m - 1)
                out = ps_p[k % 2][:].rearrange("p (s q) -> p s q", q=PR)
                nc.tensor.matmul(out, bs_parts[:], sc_parts[:].rearrange("p (s q) -> p s q", s=1).broadcast_to(
                    [PARTS * PARTS, SPB, PR]), start=True, stop=True, skip_group_check=True)
                for c, b0, o0, nb in pieces:
                    mm = nc.tensor.matmul(out[:, o0:o0 + nb, :], y_norm[:, c, :],
                                          wsi_c[:, SPC * (c % PERIOD) + b0:SPC * (c % PERIOD) + b0 + nb, :],
                                          start=False, stop=True, skip_group_check=True)
                mm.then_inc(bank_projected, 1)

            def z_step(i, s):
                pe.wait_ge(p_hat_ready, BANKS * i + 2 * s + 2)
                if behind(i, s, 1):
                    pe.wait_ge(z_copied, ZSTEPS * i + s)
                for g in range(GZ):
                    for j in range(J):
                        b = J * (s * GZ + g) + j
                        mm = nc.tensor.matmul(ps_z[PR * j:PR * j + PR, g * NZ:(g + 1) * NZ],
                                              items[:, b, 2:IW], items[:, b, 0:NZ], start=True, stop=True)
                mm.then_inc(z_ready, 1)

            def fold_sums(qb):
                if qb == 0:
                    pe.wait_ge(wl_loaded, 16 * (QB // WL_PIECE + 1))
                mm = nc.tensor.matmul(ps_m[:], bsi_fold_sb[:, qb, :], wl_sb[:, qb, :],
                                      start=(qb == 0), stop=(qb == QB - 1))
                if qb == QB - 1:
                    mm.then_inc(sums_folded, 1)

            def fold_const():
                pe.wait_ge(sums_taken, 1)
                nc.tensor.matmul(ps_m[:], bsi_col_sb[:], sum_raw[:], start=True, stop=True
                                 ).then_inc(const_folded, 1)

            def interact(i, part):
                if part == 0:
                    pe.wait_ge(z_regrouped_act, REGROUPED_ACT * (i + 1))
                    pe.wait_ge(z_regrouped_dve, REGROUPED_DVE * (i + 1))
                n = -(-QB // len(LAG_INTERACT))
                for q in range(n * part, min(n * part + n, QB)):
                    mm = nc.tensor.matmul(ps_m[:], z_qp[:, :, :, q].rearrange("p j g -> p (j g)"),
                                          wl_sb[:, q, :], start=(q == 0), stop=(q == QB - 1))
                if q == QB - 1:
                    mm.then_inc(o_ready, 1)

            def turn_out(i):
                pe.wait_ge(o_hat_ready, i + 1)
                for c in range(ZK):
                    mm = nc.tensor.transpose(ps_m[:, c * P:(c + 1) * P], o_hat[:, c * P:(c + 1) * P], eye_sb[:])
                mm.then_inc(o_turned, 1)

            def layer_1(i, part):
                n = HK // len(LAG_LAYER_1)
                if part == 0:
                    pe.wait_ge(z_t_ready, ZK * (i + 1))
                else:
                    pe.wait_ge(h1_ready, HK * i + n * part)
                for m in range(n * part, n * part + n):
                    for c in range(ZK + DK):
                        rhs = z_t[:, c, :] if c < ZK else dense_sb[:, c - ZK, bass.ds(i * P, P)]
                        mm = nc.tensor.matmul(ps_m[:, m * P:(m + 1) * P], w1_sb[:, c, m * P:(m + 1) * P], rhs,
                                              start=(c == 0), stop=(c == ZK + DK - 1))
                mm.then_inc(h1_summed, 1)

            def layer_2(i):
                pe.wait_ge(h1_ready, HK * (i + 1))
                for m in range(H2 // P):
                    for c in range(HK):
                        mm = nc.tensor.matmul(ps_m[:, m * P:(m + 1) * P], w2_sb[:, c, m * P:(m + 1) * P],
                                              h1_t[:, c, :], start=(c == 0), stop=(c == HK - 1))
                mm.then_inc(h2_summed, 1)

            def layer_3(i):
                pe.wait_ge(h2_ready, H2 // P * (i + 1))
                for c in range(H2 // P):
                    mm = nc.tensor.matmul(ps_m[0:1, 0:P], w3_sb[:, c:c + 1], h2_t[:, c, :],
                                          start=(c == 0), stop=(c == H2 // P - 1))
                mm.then_inc(y_summed, 1)

            def step(i, t, own, before):
                for tile, u in lagged(i, t, LAG_TURN, own, before):
                    turn_pair(tile, u)
                for tile, u in lagged(i, t, LAG_EMBED, own, before):
                    embed_pair(tile, u)
                for tile, u in lagged(i, t, LAG_PROJECT, own, before):
                    for k in bank_after(u):
                        project_bank(tile, k)
                for lag, work in ((LAG_TURN_OUT, turn_out), (LAG_LAYER_2, layer_2)):
                    for tile, u in lagged(i, t, lag, own, before):
                        if u == PAIRS - 1:
                            work(tile)
                for tile, u in lagged(i, t, LAG_Z, own, before):
                    for s in z_after(u):
                        z_step(tile, s)
                for part, lag in enumerate(LAG_INTERACT):
                    for tile, u in lagged(i, t, lag, own, before):
                        if u == PAIRS - 1:
                            interact(tile, part)
                for part, lag in enumerate(LAG_LAYER_1):
                    for tile, u in lagged(i, t, lag, own, before):
                        if u == PAIRS - 1:
                            layer_1(tile, part)
                for tile, u in lagged(i, t, LAG_LAYER_2, own, before):
                    if u == PAIRS - 1:
                        layer_3(tile)

            for t in range(PAIRS):
                if t == LAG_PROJECT + 1:
                    pe.wait_ge(weights_ready, 2)
                if t == LAG_Z + 3:
                    pe.wait_ge(x_summed, 1)
                step(0, t, True, False)
                if t == DENSE_AT[0] - 1:
                    project_dense()
                if t == DENSE_AT[1]:
                    turn_dense()
                if t == DENSE_AT[2]:
                    sum_dense()
                if t >= FOLD_AT:
                    for qb in range(2 * (t - FOLD_AT), min(QB, 2 * (t - FOLD_AT + 1))):
                        fold_sums(qb)
                if t == FOLD_AT + FOLD_STEPS + 1:
                    fold_const()
            pe.wait_ge(top_loaded, 48)
            with pe.Fori(1, TILES) as i:
                for t in range(PAIRS):
                    step(i, t, True, True)
            for t in range(PAIRS):
                step(TILES, t, False, True)


def kernel(**inputs):
    import concourse.bacc as bacc
    from concourse.bass_utils import run_bass_kernel_spmd

    a = {k: np.asarray(v) for k, v in inputs.items()}
    arrays = {}

    base = np.concatenate([[0], np.cumsum(VOCAB)[:-1]]).astype(np.int32)
    rows = np.stack([a["ids"].reshape(-1), np.tile(base, B)])
    arrays["rows_at"] = np.ascontiguousarray(rows.reshape(2, TILES * CH, P).transpose(2, 0, 1))
    arrays["tables"] = np.concatenate([a[f"tbl_{t}"] for t in range(NT)], axis=0)

    consts = {}
    dense = a["r_dense_t"].T.reshape(DK, P, TILES, G, J).transpose(1, 0, 2, 4, 3)

    def k_major(w, k):
        return np.ascontiguousarray(w.reshape(k, P, -1).transpose(1, 0, 2))

    dense = np.concatenate([dense.reshape(P, DK, B), k_major(a["L0_rec_Wd"].T, DK)], axis=2)
    consts["gd"], consts["bd"] = a["L0_rec_gd"], a["L0_rec_bd"]
    consts["ws"] = np.zeros((2, D, 2, E), np.float32)
    for r in range(2):
        consts["ws"][r, :, r] = a["L0_rec_Ws"].T
    consts["gs"] = np.tile(a["L0_rec_gs"], (P, 1))
    consts["bs"] = np.tile(a["L0_rec_bs"], (PARTS * PARTS, 1))

    wsi_t = np.ascontiguousarray(a["L0_rec_Wsi"].T)
    wsi_rows = np.zeros((P, PERIOD, PR), np.float32)
    row_sample = np.zeros((P, PERIOD, SPC), np.float32)
    for c in range(PERIOD):
        for r in range(P):
            sample, table = divmod(P * c + r, NT)
            wsi_rows[r, c] = wsi_t[table]
            row_sample[r, c, sample - chunk_samples(c)[0]] = 1
    consts["wsi_rows"] = wsi_rows.reshape(P, -1)
    consts["row_sample"] = row_sample.reshape(P, -1)
    arrays["dense"] = dense
    consts["wsi_t"] = wsi_t

    gsi, bsi, wl_t = a["L0_rec_gsi"], a["L0_rec_bsi"], a["L0_rec_Wl"].T
    slots = np.zeros((QA * QB, PR, MD), np.float32)
    gsi_q = np.ones((QA * QB, PR), np.float32)
    fold = np.zeros((QA * QB, PR, P), np.float32)
    dense_row = PR * DENSE_SUM_SLOT[0]
    for n, (hi, lo) in enumerate(zip(*np.tril_indices(NI, k=-1))):
        p, slot = hi - 1, lo + 1 if lo else 0
        slots[slot, p] = wl_t[n]
        if lo:
            fold[slot, p, p] = bsi[lo - 1]
            fold[slot, p, lo - 1] = bsi[p]
        else:
            fold[slot, p, dense_row] = bsi[p]
    for q in range(PR - 1):
        gsi_q[q + 2] = gsi[q]
    consts["gsi_p"] = np.ascontiguousarray(np.tile(gsi, QA).reshape(P, 1))
    consts["gsi_q"] = np.ascontiguousarray(gsi_q.reshape(QA, QB, PR).transpose(0, 2, 1)).reshape(P, QB)
    consts["bsi_col"] = np.zeros((PR, P), np.float32)
    consts["bsi_col"][:, dense_row] = bsi
    bsi_fold = np.ascontiguousarray(fold.reshape(QA, QB, PR, P).transpose(0, 2, 1, 3)
                                              ).reshape(P, QB, P)
    slots = slots.reshape(QA, QB, PR, MD).transpose(0, 2, 1, 3)
    arrays["wl_slots"] = np.ascontiguousarray(slots).reshape(P, QB, MD)
    arrays["bsi_fold"] = bsi_fold
    consts["gl"] = np.ascontiguousarray(a["L0_rec_gl"][:USED].reshape(ZK, P).T)
    consts["bl"] = np.ascontiguousarray(a["L0_rec_bl"][:USED].reshape(ZK, P).T)

    w1 = a["W_top1"]
    arrays["w1"] = k_major(np.concatenate([w1[:USED], w1[MD:]], axis=0), ZK + DK)
    consts["b1"] = np.ascontiguousarray(a["b_top1"].reshape(HK, P).T)
    arrays["w2"] = k_major(a["W_top2"], HK)
    consts["b2"] = np.ascontiguousarray(a["b_top2"].reshape(H2 // P, P).T)
    consts["w3"] = np.ascontiguousarray(a["W_top3"].reshape(H2 // P, P).T)

    consts["eye"] = np.eye(P, dtype=np.float32)
    masks = np.zeros((PARTS * PARTS, 2 * PARTS), np.float32)
    for r in range(PARTS * PARTS):
        masks[r, r // PARTS] = 1
        masks[r, PARTS + r % PARTS] = 1
    consts["part_masks"] = masks

    packed = {}
    for name, width in CONSTS.items():
        part = np.asarray(consts[name]).reshape(-1, width)
        packed[name] = np.zeros((P, width), np.float32)
        packed[name][:len(part)] = part
    arrays["consts"] = np.concatenate(list(packed.values()), axis=1)
    order = ("rows_at", "tables", "consts", "dense", "wl_slots", "bsi_fold", "w1", "w2")
    arrays = {name: arrays[name] for name in order}

    nc = bacc.Bacc("TRN2", target_bir_lowering=False, num_devices=1)
    args = [nc.dram_tensor(f"in_{k}", v.shape, mybir.dt.from_np(v.dtype), kind="ExternalInput").ap()
            for k, v in arrays.items()]
    y_out = nc.dram_tensor("y_out", (1, B), F32, kind="ExternalOutput").ap()
    build(nc, *args, y_out)
    r = run_bass_kernel_spmd(nc, [{f"in_{k}": v for k, v in arrays.items()}], core_ids=[0])
    return r.results[0]["y_out"].reshape(B, 1)
```
